# Optimizing a Trainium2 kernel written in Bass

```python
import numpy as np
import jax
import jax.numpy as jnp

def _softmax(x, axis=-1):
    return jax.nn.softmax(x, axis=axis)

def _gelu(x):
    return jax.nn.gelu(x, approximate=True)

def _silu(x):
    return jax.nn.silu(x)

def _sigmoid(x):
    return jax.nn.sigmoid(x)

def _layernorm(x, axis=-1, eps=1e-05):
    m = jnp.mean(x, axis=axis, keepdims=True)
    v = jnp.var(x, axis=axis, keepdims=True)
    return (x - m) / jnp.sqrt(v + eps)

def _scatter_add(tgt, idx, src, axis=0):
    return tgt.at[idx].add(src)

def _segment_sum(src, seg, n):
    return jax.ops.segment_sum(src, seg, n)
kernel_name = 'mk_conv_attn_hybrid_d2_conv_nhwc512_r4_b99737'

def setup_inputs(seed: int=0):
    np.random.seed(seed)
    _w = jnp.asarray

    def _rec_inputs():
        import jax
        import jax.numpy as jnp
        _gk = jax.random.key(seed)
        x = -0.0003929 + 0.9999 * jax.random.normal(jax.random.fold_in(_gk, 1), (8, 16, 16, 128), jnp.float32)
        return x
    x = _rec_inputs()

    def _L0_conv_setup():
        import jax, jax.numpy as jnp
        import numpy as np
        B, H, W, C = (8, 16, 16, 128)
        D = C // 8
        key = jax.random.key(seed)
        ks = jax.random.split(key, 5)
        scale = 1.0 / np.sqrt(C)
        return {'x': jax.random.normal(ks[0], (B, H, W, C), dtype=jnp.float32), 'Wf': jax.random.normal(ks[1], (C, D), dtype=jnp.float32) * scale, 'bf': jnp.zeros((D,), dtype=jnp.float32), 'Wg': jax.random.normal(ks[2], (C, D), dtype=jnp.float32) * scale, 'bg': jnp.zeros((D,), dtype=jnp.float32), 'Wh': jax.random.normal(ks[3], (C, D), dtype=jnp.float32) * scale, 'bh': jnp.zeros((D,), dtype=jnp.float32), 'Wv': jax.random.normal(ks[4], (D, C), dtype=jnp.float32) * (1.0 / np.sqrt(D)), 'bv': jnp.zeros((C,), dtype=jnp.float32), 'gamma': jnp.float32(0.01)}
    _L0_conv_all = _L0_conv_setup()
    _L0_conv_in = {k: v for k, v in _L0_conv_all.items() if k in ('Wf', 'bf', 'Wg', 'bg', 'Wh', 'bh', 'Wv', 'bv', 'gamma')}
    del _L0_conv_all

    def _L1_attn_setup():
        import jax, jax.numpy as jnp
        import numpy as np
        EMBED_DIM = 128
        NUM_HEADS = 8
        D_K = EMBED_DIM // NUM_HEADS
        FFN_DIM = 512
        N_QUBITS_FFN = 8
        LN_EPS = 1e-05

        def _layernorm(x, g, b):
            mu = jnp.mean(x, axis=-1, keepdims=True)
            var = jnp.var(x, axis=-1, keepdims=True)
            return (x - mu) * jax.lax.rsqrt(var + LN_EPS) * g + b

        def _attn_quantum(h, theta):
            c = jnp.cos(h + theta)
            cp = jnp.cumprod(c, axis=-1)
            z0 = jnp.prod(c[..., 1:], axis=-1)
            return cp.at[..., 0].set(z0)
        key = jax.random.key(seed)
        ks = jax.random.split(key, 10)
        B, S = (2, 512)
        return {'x': jax.random.normal(ks[0], (B, S, EMBED_DIM), dtype=jnp.float32), 'theta_attn': jax.random.normal(ks[1], (D_K,), dtype=jnp.float32) * 0.1, 'phi_ffn': jax.random.normal(ks[2], (N_QUBITS_FFN,), dtype=jnp.float32) * 0.1, 'W_comb': jax.random.normal(ks[3], (EMBED_DIM, EMBED_DIM), dtype=jnp.float32) * 0.02, 'b_comb': jnp.zeros((EMBED_DIM,), dtype=jnp.float32), 'W1': jax.random.normal(ks[4], (FFN_DIM, N_QUBITS_FFN), dtype=jnp.float32) * 0.1, 'b1': jnp.zeros((FFN_DIM,), dtype=jnp.float32), 'W2': jax.random.normal(ks[5], (EMBED_DIM, FFN_DIM), dtype=jnp.float32) * 0.02, 'b2': jnp.zeros((EMBED_DIM,), dtype=jnp.float32), 'ln1_g': jnp.ones((EMBED_DIM,), dtype=jnp.float32), 'ln1_b': jnp.zeros((EMBED_DIM,), dtype=jnp.float32), 'ln2_g': jnp.ones((EMBED_DIM,), dtype=jnp.float32), 'ln2_b': jnp.zeros((EMBED_DIM,), dtype=jnp.float32)}
    _L1_attn_all = _L1_attn_setup()
    _L1_attn_in = {k: v for k, v in _L1_attn_all.items() if k in ('theta_attn', 'phi_ffn', 'W_comb', 'b_comb', 'W1', 'b1', 'W2', 'b2', 'ln1_g', 'ln1_b', 'ln2_g', 'ln2_b')}
    del _L1_attn_all

    def _L1_ffn_setup():
        import jax, jax.numpy as jnp
        import numpy as np
        TOP_K = 2
        key = jax.random.key(seed)
        k1, k2, k3, k4 = jax.random.split(key, 4)
        B, S, d = (4, 512, 128)
        E, H = (32, 32)
        x = jax.random.normal(k1, (B, S, d), dtype=jnp.float32)
        expert_sel = jax.random.normal(k2, (E, d), dtype=jnp.float32) / np.sqrt(d).astype(np.float32)
        keys = jax.random.normal(k3, (E, d, H), dtype=jnp.float32) / np.sqrt(d).astype(np.float32)
        values = jax.random.normal(k4, (E, H, d), dtype=jnp.float32) / np.sqrt(E * H).astype(np.float32)
        return {'x': x, 'expert_sel': expert_sel, 'keys': keys, 'values': values}
    _L1_ffn_all = _L1_ffn_setup()
    _L1_ffn_in = {k: v for k, v in _L1_ffn_all.items() if k in ('expert_sel', 'keys', 'values')}
    del _L1_ffn_all
    return {'x': x, 'L0_conv_Wf': _L0_conv_in['Wf'], 'L0_conv_bf': _L0_conv_in['bf'], 'L0_conv_Wg': _L0_conv_in['Wg'], 'L0_conv_bg': _L0_conv_in['bg'], 'L0_conv_Wh': _L0_conv_in['Wh'], 'L0_conv_bh': _L0_conv_in['bh'], 'L0_conv_Wv': _L0_conv_in['Wv'], 'L0_conv_bv': _L0_conv_in['bv'], 'L0_conv_gamma': _L0_conv_in['gamma'], 'L1_attn_theta_attn': _L1_attn_in['theta_attn'], 'L1_attn_phi_ffn': _L1_attn_in['phi_ffn'], 'L1_attn_W_comb': _L1_attn_in['W_comb'], 'L1_attn_b_comb': _L1_attn_in['b_comb'], 'L1_attn_W1': _L1_attn_in['W1'], 'L1_attn_b1': _L1_attn_in['b1'], 'L1_attn_W2': _L1_attn_in['W2'], 'L1_attn_b2': _L1_attn_in['b2'], 'L1_attn_ln1_g': _L1_attn_in['ln1_g'], 'L1_attn_ln1_b': _L1_attn_in['ln1_b'], 'L1_attn_ln2_g': _L1_attn_in['ln2_g'], 'L1_attn_ln2_b': _L1_attn_in['ln2_b'], 'L1_ffn_expert_sel': _L1_ffn_in['expert_sel'], 'L1_ffn_keys': _L1_ffn_in['keys'], 'L1_ffn_values': _L1_ffn_in['values']}

def reference(x, L0_conv_Wf, L0_conv_bf, L0_conv_Wg, L0_conv_bg, L0_conv_Wh, L0_conv_bh, L0_conv_Wv, L0_conv_bv, L0_conv_gamma, L1_attn_theta_attn, L1_attn_phi_ffn, L1_attn_W_comb, L1_attn_b_comb, L1_attn_W1, L1_attn_b1, L1_attn_W2, L1_attn_b2, L1_attn_ln1_g, L1_attn_ln1_b, L1_attn_ln2_g, L1_attn_ln2_b, L1_ffn_expert_sel, L1_ffn_keys, L1_ffn_values):
    import jax
    import jax.numpy as jnp

    def _L0_conv_ref(x, Wf, bf, Wg, bg, Wh, bh, Wv, bv, gamma):
        import jax, jax.numpy as jnp
        import numpy as np
        B, H, W, C = (8, 16, 16, 128)
        D = C // 8
        b, h, w, c = x.shape
        n = h * w
        xf = x.reshape(b, n, c)
        f = xf @ Wf + bf
        g = xf @ Wg + bg
        hh = xf @ Wh + bh
        s = jnp.einsum('bnd,bmd->bnm', f, g)
        attn = jax.nn.softmax(s, axis=-1)
        context = jnp.einsum('bnm,bmd->bnd', attn, hh)
        o = gamma * context @ Wv + bv + xf
        return o.reshape(b, h, w, c)

    def _L1_attn_ref(x, theta_attn, phi_ffn, W_comb, b_comb, W1, b1, W2, b2, ln1_g, ln1_b, ln2_g, ln2_b):
        import jax, jax.numpy as jnp
        import numpy as np
        EMBED_DIM = 128
        NUM_HEADS = 8
        D_K = EMBED_DIM // NUM_HEADS
        FFN_DIM = 512
        N_QUBITS_FFN = 8
        LN_EPS = 1e-05

        def _layernorm(x, g, b):
            mu = jnp.mean(x, axis=-1, keepdims=True)
            var = jnp.var(x, axis=-1, keepdims=True)
            return (x - mu) * jax.lax.rsqrt(var + LN_EPS) * g + b

        def _attn_quantum(h, theta):
            c = jnp.cos(h + theta)
            cp = jnp.cumprod(c, axis=-1)
            z0 = jnp.prod(c[..., 1:], axis=-1)
            return cp.at[..., 0].set(z0)
        B, S, E = x.shape
        H, d = (NUM_HEADS, D_K)
        h = x.reshape(B, S, H, d)
        proj = _attn_quantum(h, theta_attn)
        proj = proj.transpose(0, 2, 1, 3)
        scores = jnp.einsum('bhsd,bhtd->bhst', proj, proj) / jnp.sqrt(jnp.float32(d))
        attn = jax.nn.softmax(scores, axis=-1)
        ctx = jnp.einsum('bhst,bhtd->bhsd', attn, proj)
        ctx = ctx.transpose(0, 2, 1, 3).reshape(B, S, E)
        attn_out = ctx @ W_comb.T + b_comb
        x1 = _layernorm(x + attn_out, ln1_g, ln1_b)
        q = jnp.cos(x1[..., :N_QUBITS_FFN]) * jnp.cos(phi_ffn)
        hid = jax.nn.relu(q @ W1.T + b1)
        ffn_out = hid @ W2.T + b2
        return _layernorm(x1 + ffn_out, ln2_g, ln2_b)

    def _L1_ffn_ref(x, expert_sel, keys, values):
        import jax, jax.numpy as jnp
        import numpy as np
        TOP_K = 2
        B, S, d = x.shape
        E = keys.shape[0]
        xt = x.reshape(-1, d)
        T = xt.shape[0]
        sel = jax.nn.sigmoid(xt @ expert_sel.T)
        sel_val, sel_idx = jax.lax.top_k(sel, TOP_K)
        w = jnp.zeros((T, E), dtype=xt.dtype).at[jnp.arange(T)[:, None], sel_idx].add(sel_val)
        h = jax.nn.relu(jnp.einsum('td,edh->teh', xt, keys))
        out = jnp.einsum('teh,te,ehv->tv', h, w, values)
        return out.reshape(B, S, -1)

    def _gn(v, G=32, eps=1e-05):
        B_, H_, W_, C_ = v.shape
        g = v.reshape(B_, H_, W_, G, C_ // G)
        m = jnp.mean(g, axis=(1, 2, 4), keepdims=True)
        s = jnp.var(g, axis=(1, 2, 4), keepdims=True)
        return ((g - m) / jnp.sqrt(s + eps)).reshape(v.shape)

    def _ln_c(v, eps=1e-06):
        m = jnp.mean(v, axis=-1, keepdims=True)
        s = jnp.var(v, axis=-1, keepdims=True)
        return (v - m) / jnp.sqrt(s + eps)

    def _ln_t(v, eps=1e-05):
        m = jnp.mean(v, axis=-1, keepdims=True)
        s = jnp.var(v, axis=-1, keepdims=True)
        return (v - m) / jnp.sqrt(s + eps)

    def _to_tokens(v):
        B_, H_, W_, C_ = v.shape
        return v.reshape(B_, H_ * W_, C_)

    def _from_tokens(t, like):
        return t.reshape(like.shape)
    x = _L0_conv_ref(x, L0_conv_Wf, L0_conv_bf, L0_conv_Wg, L0_conv_bg, L0_conv_Wh, L0_conv_bh, L0_conv_Wv, L0_conv_bv, L0_conv_gamma)
    t = _to_tokens(x)
    t = t + _L1_attn_ref(_ln_t(t), L1_attn_theta_attn, L1_attn_phi_ffn, L1_attn_W_comb, L1_attn_b_comb, L1_attn_W1, L1_attn_b1, L1_attn_W2, L1_attn_b2, L1_attn_ln1_g, L1_attn_ln1_b, L1_attn_ln2_g, L1_attn_ln2_b)
    t = t + _L1_ffn_ref(_ln_t(t), L1_ffn_expert_sel, L1_ffn_keys, L1_ffn_values)
    x = _from_tokens(t, x)
    return x

_drawn_inputs = setup_inputs


def setup_inputs(seed=0):
    import zlib

    import numpy as np

    out = dict(_drawn_inputs(seed))
    spreads = {'L0_conv_bf': (0.0, 0.8),
     'L0_conv_bg': (0.0, 2.0),
     'L0_conv_bh': (0.0, 0.8),
     'L0_conv_bv': (0.0, 0.1),
     'L1_attn_b_comb': (0.0, 0.1),
     'L1_attn_b1': (0.0, 0.389),
     'L1_attn_b2': (0.0, 0.1),
     'L1_attn_ln1_g': (1.0, 0.2),
     'L1_attn_ln1_b': (0.0, 0.1),
     'L1_attn_ln2_g': (1.0, 0.2),
     'L1_attn_ln2_b': (0.0, 0.1)}
    factors = {'L0_conv_Wf': 6.237,
     'L0_conv_Wg': 5.915,
     'L0_conv_Wh': 6.537,
     'L0_conv_Wv': 6.364,
     'L1_attn_theta_attn': 21.67,
     'L1_attn_phi_ffn': 48.423,
     'L1_attn_W_comb': 20.21}
    for name, (base, spread) in spreads.items():
        noise = np.random.default_rng([zlib.crc32(name.encode()), seed]).standard_normal(out[name].shape)
        drawn = base * np.exp(spread * noise) if base else spread * noise
        out[name] = jnp.asarray(drawn.astype(out[name].dtype))
    for name, factor in factors.items():
        out[name] = (out[name] * factor).astype(out[name].dtype)
    return out
```

```python
from contextlib import ExitStack
import math

import concourse.bass as bass
from concourse import mybir

F32 = mybir.dt.float32
BF16 = mybir.dt.bfloat16
F16 = mybir.dt.float16
U32 = mybir.dt.uint32
ALU = mybir.AluOpType
ACT = mybir.ActivationFunctionType
AX = mybir.AxisListType

P = 128
ROUND = 1.5 * 2.0 ** 23
TWO_PI_HI = 6.28125
TWO_PI_LO = 2.0 * math.pi - TWO_PI_HI
PI_F32 = 3.1415925
EPS = 1e-5

START = {
    "conv_transpose": 0.000, "conv_project": 0.043, "conv_stack": 0.271, "conv_scores": 0.414, "conv_turn": 0.661,
    "conv_output": 0.892,
    "proj_norm": 1.182, "proj_angle": 1.440, "proj_reduce": 1.557, "proj_cos": 1.726, "proj_split": 1.894,
    "attn_transpose": 2.115, "attn_scores0": 2.188, "attn_scores1": 2.230, "attn_scores2": 2.324,
    "attn_scores3": 2.328, "attn_context0": 2.411, "attn_scores4": 2.580, "attn_scores5": 2.604,
    "attn_scores6": 2.628, "attn_scores7": 2.665, "attn_context1": 2.790, "attn_turn": 2.874, "attn_back": 2.942,
    "attn_combine": 2.996,
    "ffn_norm": 3.243, "ffn_angle": 3.493, "ffn_cos": 3.723, "ffn_transpose": 3.974, "ffn_hidden0": 4.094,
    "ffn_hidden1": 4.331, "ffn_output": 4.628,
    "norm_second": 4.704, "norm_third": 4.941,
    "moe_transpose": 5.240, "moe_select": 5.295, "moe_topk": 5.481, "moe_spread": 5.686, "moe_pair0": 5.734,
    "moe_pair1": 5.899, "moe_pair2": 5.962, "moe_pair3": 6.080, "moe_output": 6.187,
}


PACE = {"conv": 0.991, "proj": 1.000, "attn": 1.000, "ffn": 1.000, "norm": 1.000, "moe": 1.000}


def build(nc, x, Wf, bf, Wg, bg, Wh, bh, Wv, bv, gamma, theta, phi, W_comb, b_comb, W1, b1, W2, b2,
          ln1_g, ln1_b, ln2_g, ln2_b, expert_sel, keys, values, out):
    NB, IH, IW, C = x.shape
    N = IH * IW
    TB = N // P
    D = Wf.shape[1]
    DK = theta.shape[0]
    H = C // DK
    FF, NQ = W1.shape
    FB = FF // P
    E, _, HE = keys.shape
    EB = E * HE // P
    EPB = P // HE
    assert C == P and D == DK == 16 and TB == 2 and 2 * N == 512 and E * 3 == 96
    xv = x.rearrange("b h w c -> b (h w) c").rearrange("b (t p) c -> b p t c", p=P)
    ov = out.rearrange("b h w c -> b (h w) c").rearrange("b (t p) c -> b p t c", p=P)

    with ExitStack() as es:
        def sb(name, shape, dt=F32):
            return es.enter_context(nc.sbuf_tensor(name, shape, dt))

        def ps(name, dt=F32):
            return es.enter_context(nc.psum_tensor(name, [P, 2048 // (4 if dt == F32 else 2)], dt))

        def sem(name):
            return es.enter_context(nc.semaphore(name))

        s_ident = sem("s_ident")
        s_spread_set = sem("s_spread_set")
        s_zeroed = sem("s_zeroed")
        s_ones_set = sem("s_ones_set")
        s_const_set = sem("s_const_set")
        s_wproj_sb = sem("s_wproj_sb")
        s_whT_ps = sem("s_whT_ps")
        s_whT = sem("s_whT")
        s_wv_ps = sem("s_wv_ps")
        s_rc_ps = sem("s_rc_ps")
        s_rc = sem("s_rc")
        s_bh_row = sem("s_bh_row")
        s_b1T_ps = sem("s_b1T_ps")
        s_wcT_ps = sem("s_wcT_ps")
        s_wcT = sem("s_wcT")
        s_w2T_ps = sem("s_w2T_ps")
        s_w2T = sem("s_w2T")
        s_selT_ps = sem("s_selT_ps")
        s_selT = sem("s_selT")
        s_phi_step = sem("s_phi_step")
        s_phi_clamp = sem("s_phi_clamp")
        s_phi_cos = sem("s_phi_cos")
        s_w1_step = sem("s_w1_step")
        s_w1_stack = sem("s_w1_stack")
        s_w1T_ps = sem("s_w1T_ps")
        s_w1T = sem("s_w1T")
        s_theta2 = sem("s_theta2")
        s_xT_ps = sem("s_xT_ps")
        s_xT = sem("s_xT")
        s_proj_ps = sem("s_proj_ps")
        s_fg = sem("s_fg")
        s_hW = sem("s_hW")
        s_fg_h = sem("s_fg_h")
        s_fg_r = sem("s_fg_r")
        s_fg_m = sem("s_fg_m")
        s_fg_l = sem("s_fg_l")
        s_stack_ps = sem("s_stack_ps")
        s_stack = sem("s_stack")
        s_cscore_ps = sem("s_cscore_ps")
        s_cmax = sem("s_cmax")
        s_cexp = sem("s_cexp")
        s_ET_ps = sem("s_ET_ps")
        s_ET = sem("s_ET")
        s_O_ps = sem("s_O_ps")
        s_xr = sem("s_xr")
        s_crden = sem("s_crden")
        s_cgain = sem("s_cgain")
        s_t0 = sem("s_t0")
        s_y_stats = sem("s_y_stats")
        s_y_mv = sem("s_y_mv")
        s_y_var = sem("s_y_var")
        s_y_rstd = sem("s_y_rstd")
        s_y = sem("s_y")
        s_y_arg = sem("s_y_arg")
        s_y_k1 = sem("s_y_k1")
        s_y_k = sem("s_y_k")
        s_y_r1 = sem("s_y_r1")
        s_y_r2 = sem("s_y_r2")
        s_y_clamp = sem("s_y_clamp")
        s_y_cos = sem("s_y_cos")
        s_y_bias = sem("s_y_bias")
        s_scan = sem("s_scan")
        s_p_aug = sem("s_p_aug")
        s_left_h = sem("s_left_h")
        s_left_l = sem("s_left_l")
        s_right = sem("s_right")
        s_LT_ps = sem("s_LT_ps")
        s_LT = sem("s_LT")
        s_RT_ps = sem("s_RT_ps")
        s_RT = sem("s_RT")
        s_score_ps = sem("s_score_ps")
        s_prob = sem("s_prob")
        s_ctx_ps = sem("s_ctx_ps")
        s_CT = sem("s_CT")
        s_CTT_ps = sem("s_CTT_ps")
        s_arden = sem("s_arden")
        s_ctx = sem("s_ctx")
        s_ctxT_ps = sem("s_ctxT_ps")
        s_ctxT = sem("s_ctxT")
        s_comb_ps = sem("s_comb_ps")
        s_z = sem("s_z")
        s_z_stats = sem("s_z_stats")
        s_z_mv = sem("s_z_mv")
        s_z_var = sem("s_z_var")
        s_z_rstd = sem("s_z_rstd")
        s_z_n = sem("s_z_n")
        s_x1 = sem("s_x1")
        s_x1_bias = sem("s_x1_bias")
        s_q_arg = sem("s_q_arg")
        s_q_k1 = sem("s_q_k1")
        s_q_k = sem("s_q_k")
        s_q_r1 = sem("s_q_r1")
        s_q_r2 = sem("s_q_r2")
        s_q_clamp = sem("s_q_clamp")
        s_q_cos = sem("s_q_cos")
        s_q_h = sem("s_q_h")
        s_q_r = sem("s_q_r")
        s_q_m = sem("s_q_m")
        s_q_l = sem("s_q_l")
        s_qT_ps = sem("s_qT_ps")
        s_qT = sem("s_qT")
        s_hid_ps = sem("s_hid_ps")
        s_hid = sem("s_hid")
        s_ffn_ps = sem("s_ffn_ps")
        s_z2 = sem("s_z2")
        s_n_stats = sem("s_n_stats")
        s_n_mv = sem("s_n_mv")
        s_n_var = sem("s_n_var")
        s_n_rstd = sem("s_n_rstd")
        s_n_n = sem("s_n_n")
        s_t0_bias = sem("s_t0_bias")
        s_t1 = sem("s_t1")
        s_u_stats = sem("s_u_stats")
        s_u_mv = sem("s_u_mv")
        s_u_var = sem("s_u_var")
        s_u_rstd = sem("s_u_rstd")
        s_xt = sem("s_xt")
        s_xtT_ps = sem("s_xtT_ps")
        s_xtT = sem("s_xtT")
        s_sel_ps = sem("s_sel_ps")
        s_sel_e = sem("s_sel_e")
        s_sel_1 = sem("s_sel_1")
        s_sel_s = sem("s_sel_s")
        s_top8 = sem("s_top8")
        s_top2 = sem("s_top2")
        s_rest = sem("s_rest")
        s_w = sem("s_w")
        s_w_h = sem("s_w_h")
        s_w_r = sem("s_w_r")
        s_w_m = sem("s_w_m")
        s_w_l = sem("s_w_l")
        s_wT_ps = sem("s_wT_ps")
        s_wT = sem("s_wT")
        s_gate_ps = sem("s_gate_ps")
        s_moe_ps = sem("s_moe_ps")
        s_relu = sem("s_relu")
        s_hw = sem("s_hw")
        s_out_ps = sem("s_out_ps")
        s_out_sb = sem("s_out_sb")
        x_in = [sem(f"x_in{b}") for b in range(NB)]
        stored = [sem(f"stored{i}") for i in range(2)]
        w_in = sem("w_in")
        w2_in = sem("w2_in")
        w3_in = sem("w3_in")

        ident = sb("ident", [P, P])
        identb = sb("identb", [P, P], BF16)
        identh = sb("identh", [P, P], F16)
        spread = sb("spread", [3 * E, EB, P], BF16)
        scanmask = sb("scanmask", [P, TB * C])
        minushalf = sb("minushalf", [P, TB])
        wproj = sb("wproj", [P, 2 * D + C])
        wh_sb = sb("wh_sb", [P, D])
        whT_sb = sb("whT_sb", [D, P])
        wv_sb = sb("wv_sb", [D, C])
        bh_sb = sb("bh_sb", [D, 1])
        bh_row = sb("bh_row", [D, P])
        bfg = sb("bfg", [P, 2 * D])
        bv_b = sb("bv_b", [P, C])
        gam = sb("gam", [P, 1])
        rc = sb("rc", [P, C])
        theta_b = sb("theta_b", [P, DK])
        theta2 = sb("theta2", [P, DK])
        phi_b = sb("phi_b", [P, NQ])
        phi_t = sb("phi_t", [P, 6, NQ])
        wc_sb = sb("wc_sb", [P, C])
        wcT_sb = sb("wcT_sb", [P, C])
        w2_sb = sb("w2_sb", [P, FF])
        w2T_sb = sb("w2T_sb", [P, FB, C])
        w1_sb = sb("w1_sb", [P, FB, NQ])
        b1_sb = sb("b1_sb", [FB, P])
        w1_c = sb("w1_c", [P, FB, NQ + 1])
        w1_r = sb("w1_r", [P, FB, NQ + 1])
        w1_p = sb("w1_p", [P, FB, 3, NQ + 1], BF16)
        QK = 9 * NQ + 3
        w1_st = sb("w1_st", [P, FB, QK], BF16)
        w1T_sb = sb("w1T_sb", [QK, FF], BF16)
        bc_b = sb("bc_b", [P, C])
        b2_b = sb("b2_b", [P, C])
        g1_b = sb("g1_b", [P, C])
        be1_b = sb("be1_b", [P, C])
        g2_b = sb("g2_b", [P, C])
        be2_b = sb("be2_b", [P, C])
        sel_sb = sb("sel_sb", [E, C])
        selT_sb = sb("selT_sb", [P, E])
        keys_sb = sb("keys_sb", [P, E, HE])
        val_sb = sb("val_sb", [P, EB, C])

        X = sb("X", [P, NB, TB, C])
        XR = sb("XR", [P, NB, TB, C])
        XT = sb("XT", [P, 2, N])
        HW = sb("HW", [P, 2, TB, C])
        FGs = sb("FGs", [P, NB, TB, 2 * D])
        FGr = sb("FGr", [P, NB, TB, 2 * D])
        FGp = sb("FGp", [P, 2, TB, 2, 9, D], BF16)
        FGT = sb("FGT", [P, 2, 2 * N], BF16)
        nmx = sb("nmx", [P, NB, TB])
        den = sb("den", [P, NB, TB])
        rden = sb("rden", [P, NB, TB])
        gden = sb("gden", [P, NB, TB])
        EA = sb("EA", [P, 2, TB, N])
        ETs = sb("ETs", [P, 2, TB, N])
        T0 = sb("T0", [P, NB, TB, C])
        T1 = sb("T1", [P, NB, TB, C])
        st = sb("st", [P, 4, NB, TB, 6])
        mv = sb("mv", [P, 4, NB, TB, 2])
        var = sb("var", [P, 4, NB, TB])
        rstd = sb("rstd", [P, 4, NB, TB])
        Y = sb("Y", [P, 2, TB, C])
        YB = sb("YB", [P, 4, TB, C])
        ARG = sb("ARG", [P, 2, 6, TB, C])
        CS = sb("CS", [P, 2, TB, C])
        SC = sb("SC", [P, 2, TB, C])
        PA = sb("PA", [P, 2, TB, H, 32])
        LS = sb("LS", [P, 2, TB, H, 2, 2, DK], F16)
        RS = sb("RS", [P, 2, TB, H, 2, 2, DK], F16)
        LT = sb("LT", [P, H // 2, N], F16)
        RT = sb("RT", [P, 2, H // 2, N], F16)
        EB_ = sb("EB_", [P, H, TB, N])
        CT = sb("CT", [P, 2 * N])
        ard = sb("ard", [P, 2 * H])
        CX = sb("CX", [P, TB, C])
        CXT = sb("CXT", [P, N])
        Z = sb("Z", [P, 2, TB, C])
        ZN = sb("ZN", [P, 2, TB, C])
        X1 = sb("X1", [P, 2, TB, C])
        X1B = sb("X1B", [P, 2, TB, C])
        QA = sb("QA", [P, 2, 6, TB, NQ])
        QC = sb("QC", [P, NB, TB, NQ])
        QR = sb("QR", [P, NB, TB, NQ])
        QM = sb("QM", [P, NB, TB, NQ])
        QS = sb("QS", [P, NB, TB, QK], BF16)
        QT = sb("QT", [QK, N], BF16)
        HID = sb("HID", [P, FB, N])
        Z2 = sb("Z2", [P, 2, TB, C])
        NN = sb("NN", [P, 2, TB, C])
        T0B = sb("T0B", [P, 2, TB, C])
        XTK = sb("XTK", [P, 2, TB, C])
        XTT = sb("XTT", [P, 2, N])
        SE = sb("SE", [P, NB, TB, E])
        SG = sb("SG", [P, NB, TB, E + 6])
        V8 = sb("V8", [P, NB, TB, 8])
        R8 = sb("R8", [P, NB, TB, 8])
        SR = sb("SR", [P, NB, TB, E + 6])
        W = sb("W", [P, NB, TB, E])
        WR = sb("WR", [P, NB, TB, E])
        WP = sb("WP", [P, NB, TB, 3, E], BF16)
        WT = sb("WT", [3 * E, 2, N], BF16)
        HR = sb("HR", [P, 2, 2 * N])
        HWT = sb("HWT", [P, 2, 2, N])
        OB = sb("OB", [P, 2, TB, C])

        conv_ps = ps("conv_ps")
        attn_ps = ps("attn_ps")
        sc_ps = [ps("sc0_ps"), ps("sc1_ps")]
        ffn_ps = ps("ffn_ps")
        gate_ps = ps("gate_ps")
        wide_ps = ps("wide_ps")
        moe_ps = ps("moe_ps")

        def b16(bank, dt=BF16):
            return bank[:, :].bitcast(dt)

        def tb_of(ap):
            return ap.rearrange("p (t c) -> p t c", t=TB)

        block = es.enter_context(nc.Block())

        @block.sync
        def _(sp):
            sp.dma_start(X[:, 0], xv[0]).then_inc(x_in[0], 16)
            for dst, src in ((wproj[:, 0:D], Wf), (wproj[:, D:2 * D], Wg), (wh_sb[:, :], Wh), (wv_sb[:, :], Wv),
                             (bfg[:, 0:D], bf.partition_broadcast(P)), (bfg[:, D:2 * D], bg.partition_broadcast(P))):
                sp.dma_start(dst, src).then_inc(w_in, 16)
            for b in range(1, 3):
                sp.dma_start(X[:, b], xv[b]).then_inc(x_in[b], 16)
            for dst, src in ((wc_sb[:, :], W_comb), (w2_sb[:, :], W2), (sel_sb[:, :], expert_sel), (b2_b[:, :], b2.partition_broadcast(P))):
                sp.dma_start(dst, src).then_inc(w2_in, 16)
            for b in range(3, NB):
                sp.dma_start(X[:, b], xv[b]).then_inc(x_in[b], 16)
            sp.dma_start(val_sb[:, :, :], values.rearrange("(k e) h v -> (e h) k v", k=EB)).then_inc(w3_in, 16)
            for b in range(NB):
                sp.wait_ge(s_out_sb, b + 1)
                sp.dma_start(ov[b], OB[:, b % 2]).then_inc(stored[b % 2], 16)
            for i in range(2):
                sp.wait_ge(stored[i], 16 * (NB // 2))

        W_LOADED = 16 * 11
        W2_LOADED = 16 * 11
        W3_LOADED = 16 * 2

        def run_steps(steps):
            for _, b, name in sorted((at + b * PACE[name.split("_")[0]], b, name)
                                     for name, at in START.items() for b in range(NB)):
                step = name.rstrip("0123456789")
                if name in steps:
                    steps[name](b)
                elif step in steps:
                    steps[step](b, int(name[len(step):]))

        @block.tensor
        def _(pe):
            mm, tr = nc.tensor.matmul, nc.tensor.transpose
            pe.wait_ge(w_in, W_LOADED)
            pe.wait_ge(s_ident, 6)
            tr(conv_ps[0:D, 0:P], wh_sb[:, :], ident[:, :]).then_inc(s_whT_ps, 1)
            pe.wait_ge(s_bh_row, 1)
            mm(sc_ps[0][:, 0:C], bh_row[:, :], wv_sb[:, :], start=True, stop=True).then_inc(s_rc_ps, 1)
            pe.wait_ge(s_whT, 1)
            mm(conv_ps[:, 0:C], whT_sb[:, :], wv_sb[:, :], start=True, stop=True).then_inc(s_wv_ps, 1)

            def turn_weights():
                pe.wait_ge(w2_in, W2_LOADED)
                tr(attn_ps[:, 0:P], wc_sb[:, :], ident[:, :]).then_inc(s_wcT_ps, 1)
                for k in range(FB):
                    last = tr(ffn_ps[:, k * P:(k + 1) * P], w2_sb[:, k * P:(k + 1) * P], ident[:, :])
                last.then_inc(s_w2T_ps, 1)
                tr(moe_ps[:, 0:E], sel_sb[:, :], ident[0:E, 0:E]).then_inc(s_selT_ps, 1)
                tr(wide_ps[:, 0:FB], b1_sb[:, :], ident[0:FB, 0:FB]).then_inc(s_b1T_ps, 1)
                pe.wait_ge(s_w1_stack, 5)
                for k in range(FB):
                    last = tr(b16(sc_ps[1])[0:QK, k * P:(k + 1) * P], w1_st[:, k, :], identb[:, :])
                last.then_inc(s_w1T_ps, 1)

            def conv_transpose(b):
                pe.wait_ge(x_in[b], 16)
                if b:
                    pe.wait_ge(s_t0, b)
                if b == 0:
                    pe.wait_ge(s_wproj_sb, 1)
                for t in range(TB):
                    last = tr(conv_ps[:, t * P:(t + 1) * P], X[:, b, t, :], ident[:, :])
                last.then_inc(s_xT_ps, 1)

            def conv_project(b):
                pe.wait_ge(s_xT, b + 1)
                for t in range(TB):
                    last = mm(conv_ps[:, t * (2 * D + C):(t + 1) * (2 * D + C)], XT[:, b % 2, t * P:(t + 1) * P],
                              wproj[:, :], start=True, stop=True)
                last.then_inc(s_proj_ps, 1)

            def conv_stack(b):
                pe.wait_ge(s_hW, b + 1)
                pe.wait_ge(s_fg_l, 2 * b + 2)
                for t in range(TB):
                    for side in range(2):
                        last = tr(b16(conv_ps)[:, side * N + t * P:side * N + (t + 1) * P],
                                  FGp[:, b % 2, t, side, 0:8, :].rearrange("p i d -> p (i d)"), identb[:, :])
                last.then_inc(s_stack_ps, 1)

            def conv_scores(b):
                pe.wait_ge(s_stack, b + 1)
                for t in range(TB):
                    last = mm(conv_ps[:, t * N:(t + 1) * N], FGT[:, b % 2, t * P:(t + 1) * P], FGT[:, b % 2, N:2 * N],
                              start=True, stop=True)
                last.then_inc(s_cscore_ps, 1)

            def conv_turn(b):
                pe.wait_ge(s_cexp, b + 1)
                for m in range(TB):
                    for t in range(TB):
                        last = tr(conv_ps[:, m * N + t * P:m * N + (t + 1) * P], EA[:, b % 2, t, m * P:(m + 1) * P],
                                  ident[:, :])
                last.then_inc(s_ET_ps, 1)

            def conv_output(b):
                pe.wait_ge(s_ET, b + 1)
                for t in range(TB):
                    for m in range(TB):
                        last = mm(conv_ps[:, t * C:(t + 1) * C], ETs[:, b % 2, m, t * P:(t + 1) * P],
                                  HW[:, b % 2, m, :], start=(m == 0), stop=(m == TB - 1))
                last.then_inc(s_O_ps, 1)
                if b == 0:
                    turn_weights()

            def attn_transpose(b):
                if b == 0:
                    pe.wait_ge(s_wcT, 1)
                    pe.wait_ge(s_rc, 1)
                    pe.wait_ge(s_w1T, 1)
                if b:
                    pe.wait_ge(s_z, b)
                pe.wait_ge(s_left_l, b + 1)
                pe.wait_ge(s_right, 2 * b + 2)
                for j in range(H // 2):
                    for t in range(TB):
                        last = tr(b16(attn_ps, F16)[:, j * N + t * P:j * N + (t + 1) * P],
                                  LS[:, b % 2, t, 2 * j:2 * j + 2].rearrange("p h i j d -> p (h i j d)"), identh[:, :])
                last.then_inc(s_LT_ps, 1)
                if b >= 1:
                    pe.wait_ge(s_prob, H * b)
                for j in range(H // 2):
                    for t in range(TB):
                        last = tr(b16(sc_ps[0], F16)[:, j * N + t * P:j * N + (t + 1) * P],
                                  RS[:, b % 2, t, 2 * j:2 * j + 2].rearrange("p h i j d -> p (h i j d)"), identh[:, :])
                last.then_inc(s_RT_ps, 1)

            def attn_scores(b, h):
                pe.wait_ge(s_RT, 2 * b + 2)
                n = H * b + h
                if n >= 2:
                    pe.wait_ge(s_prob, n - 1)
                for t in range(TB):
                    last = mm(sc_ps[h % 2][:, t * N:(t + 1) * N], LT[:, h // 2, t * P:(t + 1) * P],
                              RT[:, h % 2, h // 2, :], start=True, stop=True)
                last.then_inc(s_score_ps, 1)

            def attn_context(b, g):
                pe.wait_ge(s_prob, H * b + 4 * g + 4)
                pe.wait_ge(s_LT, b + 1)
                for t in range(TB):
                    for j in range(4):
                        h = 4 * g + j
                        last = mm(attn_ps[32 * j:32 * j + 32, g * N:(g + 1) * N], PA[:, b % 2, t, h, :],
                                  EB_[:, h, t, :], start=(t == 0), stop=(t == TB - 1))
                last.then_inc(s_ctx_ps, 1)

            def attn_turn(b):
                pe.wait_ge(s_CT, b + 1)
                for t in range(TB):
                    for g in range(2):
                        last = tr(attn_ps[:, (2 * t + g) * P:(2 * t + g + 1) * P], CT[:, g * N + t * P:g * N + (t + 1) * P],
                                  ident[:, :])
                last.then_inc(s_CTT_ps, 1)

            def attn_back(b):
                pe.wait_ge(s_ctx, b + 1)
                for t in range(TB):
                    last = tr(attn_ps[:, t * P:(t + 1) * P], CX[:, t, :], ident[:, :])
                last.then_inc(s_ctxT_ps, 1)

            def attn_combine(b):
                pe.wait_ge(s_ctxT, b + 1)
                for t in range(TB):
                    last = mm(attn_ps[:, t * C:(t + 1) * C], CXT[:, t * P:(t + 1) * P], wcT_sb[:, :], start=True, stop=True)
                last.then_inc(s_comb_ps, 1)

            def ffn_transpose(b):
                if b == 0:
                    pe.wait_ge(s_w2T, 1)
                if b:
                    pe.wait_ge(s_z2, b)
                pe.wait_ge(s_q_l, b + 1)
                for t in range(TB):
                    last = tr(b16(ffn_ps)[0:QK, t * P:(t + 1) * P], QS[:, b, t, :], identb[:, :])
                last.then_inc(s_qT_ps, 1)

            def ffn_hidden(b, half):
                pe.wait_ge(s_qT, b + 1)
                if half:
                    pe.wait_ge(s_hid, 2 * b + 1)
                for i in range(2):
                    k = 2 * half + i
                    last = mm(ffn_ps[:, i * N:(i + 1) * N], w1T_sb[:, k * P:(k + 1) * P], QT[:, :], start=True, stop=True)
                last.then_inc(s_hid_ps, 1)

            def ffn_output(b):
                pe.wait_ge(s_hid, 2 * b + 2)
                for t in range(TB):
                    for k in range(FB):
                        last = mm(ffn_ps[:, t * C:(t + 1) * C], HID[:, k, t * P:(t + 1) * P], w2T_sb[:, k, :],
                                  start=(k == 0), stop=(k == FB - 1))
                last.then_inc(s_ffn_ps, 1)

            def moe_transpose(b):
                if b == 0:
                    pe.wait_ge(s_selT, 1)
                if b:
                    pe.wait_ge(s_out_sb, b)
                pe.wait_ge(s_xt, b + 1)
                for t in range(TB):
                    last = tr(moe_ps[:, t * P:(t + 1) * P], XTK[:, b % 2, t, :], ident[:, :])
                last.then_inc(s_xtT_ps, 1)

            def moe_select(b):
                pe.wait_ge(s_xtT, b + 1)
                for t in range(TB):
                    last = mm(moe_ps[:, t * E:(t + 1) * E], XTT[:, b % 2, t * P:(t + 1) * P], selT_sb[:, :],
                              start=True, stop=True)
                last.then_inc(s_sel_ps, 1)

            def moe_spread(b):
                pe.wait_ge(s_w_l, b + 1)
                pe.wait_ge(s_sel_e, b + 1)
                for t in range(TB):
                    last = tr(b16(moe_ps)[0:3 * E, t * P:(t + 1) * P], WP[:, b, t].rearrange("p i e -> p (i e)"), identb[:, :])
                last.then_inc(s_wT_ps, 1)

            def moe_out(b, q):
                pe.wait_ge(s_hw, 4 * b + q + 1)
                for t in range(TB):
                    for i in range(2):
                        k = 2 * q + i
                        last = mm(moe_ps[:, t * C:(t + 1) * C], HWT[:, q % 2, i, t * P:(t + 1) * P], val_sb[:, k, :],
                                  start=(k == 0 and t == 0), stop=(k == EB - 1), skip_group_check=True)
                last.then_inc(s_out_ps, 1)

            def moe_pair(b, q):
                n = 4 * b + q
                if n == 0:
                    pe.wait_ge(w3_in, W3_LOADED)
                    pe.wait_ge(s_spread_set, 3)
                    pe.wait_ge(s_w1_step, 5)
                if n:
                    pe.wait_ge(s_relu, n)
                for i in range(2):
                    k = 2 * q + i
                    last = mm(gate_ps[:, i * N:(i + 1) * N], keys_sb[:, k * EPB:(k + 1) * EPB, :].rearrange("p e h -> p (e h)"),
                              XTT[:, b % 2, :], start=True, stop=True)
                last.then_inc(s_gate_ps, 1)
                pe.wait_ge(s_wT, b + 1)
                if n:
                    pe.wait_ge(s_hw, n)
                for i in range(2):
                    k = 2 * q + i
                    last = mm(wide_ps[:, i * N:(i + 1) * N], spread[:, k, :], WT[:, b % 2, :], start=True, stop=True)
                last.then_inc(s_moe_ps, 1)
                if q:
                    moe_out(b, q - 1)

            def moe_output(b):
                moe_out(b, 3)

            run_steps({
                "conv_transpose": conv_transpose, "conv_project": conv_project, "conv_stack": conv_stack,
                "conv_scores": conv_scores, "conv_turn": conv_turn, "conv_output": conv_output,
                "attn_transpose": attn_transpose, "attn_scores": attn_scores, "attn_context": attn_context,
                "attn_turn": attn_turn, "attn_back": attn_back, "attn_combine": attn_combine,
                "ffn_transpose": ffn_transpose, "ffn_hidden": ffn_hidden, "ffn_output": ffn_output,
                "moe_transpose": moe_transpose, "moe_select": moe_select, "moe_spread": moe_spread,
                "moe_pair": moe_pair, "moe_output": moe_output,
            })

        @block.scalar
        def _(act):
            copy, fn = nc.scalar.copy, nc.scalar.activation
            act.dma_start(bh_sb[:, :], bh.rearrange("(d o) -> d o", o=1)).then_inc(w_in, 16)
            for dst, src in ((bv_b, bv), (gam, gamma), (theta_b, theta), (phi_b, phi)):
                act.dma_start(dst[:, :], src.partition_broadcast(P)).then_inc(w_in, 16)
            act.dma_start(w1_sb[:, :, 0:NQ], W1.rearrange("(k p) q -> p k q", p=P)).then_inc(w2_in, 16)
            act.dma_start(b1_sb[:, :], b1.rearrange("(k p) -> k p", p=P)).then_inc(w2_in, 16)
            act.dma_start(keys_sb[:, :, :], keys.rearrange("e d h -> d e h")).then_inc(w3_in, 16)
            for dst, src in ((g1_b, ln1_g), (be1_b, ln1_b), (g2_b, ln2_g), (be2_b, ln2_b), (bc_b, b_comb)):
                act.dma_start(dst[:, :], src.partition_broadcast(P)).then_inc(w2_in, 16)
            act.wait_ge(s_whT_ps, 1)
            copy(whT_sb[:, :], conv_ps[0:D, 0:P]).then_inc(s_whT, 1)
            act.wait_ge(s_wv_ps, 1)
            copy(wproj[:, 2 * D:2 * D + C], conv_ps[:, 0:C]).then_inc(s_wproj_sb, 1)
            act.wait_ge(s_phi_clamp, 1)
            fn(phi_t[:, 5, :], phi_t[:, 4, :], ACT.Sin).then_inc(s_phi_cos, 1)

            def turn_weights():
                act.wait_ge(s_wcT_ps, 1)
                copy(wcT_sb[:, :], attn_ps[:, 0:P]).then_inc(s_wcT, 1)
                act.wait_ge(s_w2T_ps, 1)
                copy(w2T_sb[:, :, :].rearrange("p k c -> p (k c)"), ffn_ps[:, :]).then_inc(s_w2T, 1)
                act.wait_ge(s_selT_ps, 1)
                copy(selT_sb[:, :], moe_ps[:, 0:E]).then_inc(s_selT, 1)
                act.wait_ge(s_w1T_ps, 1)
                copy(w1T_sb[:, :], b16(sc_ps[1])[0:QK, 0:FF]).then_inc(s_w1T, 1)

            def conv_output(b):
                if b == 0:
                    turn_weights()

            def conv_transpose(b):
                act.wait_ge(s_xT_ps, b + 1)
                copy(XT[:, b % 2, :], conv_ps[:, 0:N]).then_inc(s_xT, 1)

            def conv_project(b):
                act.wait_ge(s_fg, b + 1)
                if b >= 2:
                    act.wait_ge(s_O_ps, b - 1)
                v = conv_ps[:, 0:TB * (2 * D + C)].rearrange("p (t k) -> p t k", t=TB)
                copy(HW[:, b % 2], v[:, :, 2 * D:2 * D + C]).then_inc(s_hW, 1)

            def conv_scores(b):
                act.wait_ge(s_cmax, b + 1)
                if b >= 2:
                    act.wait_ge(s_ET_ps, b - 1)
                for t in range(TB):
                    last = fn(EA[:, b % 2, t, :], conv_ps[:, t * N:(t + 1) * N], ACT.Exp, bias=nmx[:, b, t:t + 1],
                              accum_out=den[:, b, t:t + 1])
                last.then_inc(s_cexp, 1)

            def proj_cos(b):
                act.wait_ge(s_y_clamp, b + 1)
                if b >= 2:
                    act.wait_ge(s_p_aug, 2 * (b - 1))
                fn(CS[:, b % 2], ARG[:, b % 2, 5], ACT.Sin).then_inc(s_y_cos, 1)

            def proj_split(b):
                act.wait_ge(s_p_aug, 2 * b + 2)
                if b >= 2:
                    act.wait_ge(s_LT_ps, b - 1)
                a = PA[:, b % 2].rearrange("p t h d -> p (t h) d")
                l = LS[:, b % 2].rearrange("p t h i j d -> p (t h) i j d")
                copy(l[:, :, 0], a[:, :, None, 0:DK].to_broadcast([P, TB * H, 2, DK])).then_inc(s_left_h, 1)

            def attn_scores(b, h):
                n = H * b + h
                act.wait_ge(s_score_ps, n + 1)
                if b >= 1:
                    act.wait_ge(s_ctx_ps, 2 * (b - 1) + h // 4 + 1)
                fn(EB_[:, h, :, :].rearrange("p t n -> p (t n)"), sc_ps[h % 2][:, :], ACT.Exp,
                   scale=1.0 / math.sqrt(DK)).then_inc(s_prob, 1)

            def attn_context(b, g):
                if g == 1:
                    act.wait_ge(s_ctx_ps, 2 * b + 2)
                    copy(CT[:, :], attn_ps[:, :]).then_inc(s_CT, 1)

            def attn_back(b):
                act.wait_ge(s_ctxT_ps, b + 1)
                copy(CXT[:, :], attn_ps[:, 0:N]).then_inc(s_ctxT, 1)

            def ffn_cos(b):
                act.wait_ge(s_q_clamp, b + 1)
                fn(QC[:, b], QA[:, b % 2, 5], ACT.Sin).then_inc(s_q_cos, 1)

            def ffn_hidden(b, half):
                act.wait_ge(s_hid_ps, 2 * b + half + 1)
                if b >= 1:
                    act.wait_ge(s_ffn_ps, b)
                fn(HID[:, 2 * half:2 * half + 2, :].rearrange("p k n -> p (k n)"), ffn_ps[:, :], ACT.Relu).then_inc(s_hid, 1)

            def moe_transpose(b):
                act.wait_ge(s_xtT_ps, b + 1)
                copy(XTT[:, b % 2, :], moe_ps[:, 0:N]).then_inc(s_xtT, 1)

            def moe_select(b):
                act.wait_ge(s_sel_ps, b + 1)
                fn(SE[:, b].rearrange("p t e -> p (t e)"), moe_ps[:, 0:TB * E], ACT.Exp, scale=-1.0).then_inc(s_sel_e, 1)

            def moe_pair(b, q):
                n = 4 * b + q
                act.wait_ge(s_gate_ps, n + 1)
                if n >= 2:
                    act.wait_ge(s_hw, n - 1)
                fn(HR[:, q % 2, :], gate_ps[:, :], ACT.Relu).then_inc(s_relu, 1)

            run_steps({
                "conv_transpose": conv_transpose, "conv_project": conv_project, "conv_scores": conv_scores,
                "conv_output": conv_output, "proj_split": proj_split,
                "proj_cos": proj_cos, "attn_scores": attn_scores, "attn_context": attn_context, "attn_back": attn_back,
                "ffn_cos": ffn_cos, "ffn_hidden": ffn_hidden, "moe_transpose": moe_transpose,
                "moe_select": moe_select, "moe_pair": moe_pair,
            })

        @block.vector
        def _(dve):
            V = nc.vector

            def norm_stats(b, src, which, stats, mvs):
                for t in range(TB):
                    last = V.bn_stats(st[:, which, b, t, :], src[:, t, :])
                last.then_inc(stats, 1)
                dve.wait_ge(stats, b + 1)
                for t in range(TB):
                    last = V.bn_aggr(mv[:, which, b, t, :], st[:, which, b, t, :])
                last.then_inc(mvs, 1)

            def norm_apply(b, dst, src, which, rs, done):
                dve.wait_ge(rs, b + 1)
                for t in range(TB):
                    last = V.tensor_scalar(dst[:, t, :], src[:, t, :], mv[:, which, b, t, 0:1], rstd[:, which, b, t:t + 1],
                                           ALU.subtract, ALU.mult)
                last.then_inc(done, 1)

            def norm_affine(b, dst, tmp, src, which, rs, gain, plus, half, done):
                dve.wait_ge(rs, b + 1)
                for t in range(TB):
                    V.scalar_tensor_tensor(out=tmp[:, t, :], in0=src[:, t, :], scalar=mv[:, which, b, t, 0:1],
                                           in1=gain, op0=ALU.subtract, op1=ALU.mult).then_inc(half, 1)
                for t in range(TB):
                    dve.wait_ge(half, 2 * b + t + 1)
                    last = V.scalar_tensor_tensor(out=dst[:, t, :], in0=tmp[:, t, :], scalar=rstd[:, which, b, t:t + 1],
                                                  in1=plus[t], op0=ALU.mult, op1=ALU.add)
                last.then_inc(done, 1)

            dve.wait_ge(w_in, W_LOADED)
            V.tensor_copy(bh_row[:, :], bh_sb[:, 0:1].to_broadcast([D, P])).then_inc(s_bh_row, 1)
            V.tensor_scalar(theta2[:, :], theta_b[:, :], math.pi / 2, None, ALU.add).then_inc(s_theta2, 1)
            V.tensor_scalar(phi_t[:, 0, :], phi_b[:, :], math.pi / 2, None, ALU.add).then_inc(s_phi_step, 1)
            dve.wait_ge(s_phi_step, 1)
            V.tensor_scalar(phi_t[:, 1, :], phi_t[:, 0, :], 0.5 / math.pi, ROUND, ALU.mult, ALU.add).then_inc(s_phi_step, 1)
            dve.wait_ge(s_phi_step, 2)
            V.tensor_scalar(phi_t[:, 2, :], phi_t[:, 1, :], ROUND, None, ALU.subtract).then_inc(s_phi_step, 1)
            dve.wait_ge(s_phi_step, 3)
            V.scalar_tensor_tensor(out=phi_t[:, 3, :], in0=phi_t[:, 2, :], scalar=-TWO_PI_HI, in1=phi_t[:, 0, :],
                                   op0=ALU.mult, op1=ALU.add).then_inc(s_phi_step, 1)
            dve.wait_ge(s_phi_step, 4)
            V.scalar_tensor_tensor(out=phi_t[:, 1, :], in0=phi_t[:, 2, :], scalar=-TWO_PI_LO, in1=phi_t[:, 3, :],
                                   op0=ALU.mult, op1=ALU.add).then_inc(s_phi_step, 1)
            dve.wait_ge(s_phi_step, 5)
            V.tensor_scalar(phi_t[:, 4, :], phi_t[:, 1, :], PI_F32, -PI_F32, ALU.min, ALU.max).then_inc(s_phi_clamp, 1)
            dve.wait_ge(s_rc_ps, 1)
            V.scalar_tensor_tensor(out=rc[:, :], in0=sc_ps[0][:, 0:C], scalar=gam[:, 0:1], in1=bv_b[:, :],
                                   op0=ALU.mult, op1=ALU.add).then_inc(s_rc, 1)

            def stack_w1():
                dve.wait_ge(w2_in, W2_LOADED)
                dve.wait_ge(s_phi_cos, 1)
                dve.wait_ge(s_b1T_ps, 1)
                V.tensor_copy(w1_c[:, :, NQ], wide_ps[:, 0:FB])
                V.tensor_tensor(w1_c[:, :, 0:NQ], w1_sb[:, :, :], phi_t[:, 5:6, :].to_broadcast([P, FB, NQ]),
                                ALU.mult).then_inc(s_w1_step, 1)
                dve.wait_ge(s_w1_step, 1)
                V.tensor_copy(w1_p[:, :, 0, :], w1_c[:, :, :]).then_inc(s_w1_step, 1)
                dve.wait_ge(s_w1_step, 2)
                V.tensor_tensor(w1_r[:, :, :], w1_c[:, :, :], w1_p[:, :, 0, :], ALU.subtract).then_inc(s_w1_step, 1)
                dve.wait_ge(s_w1_step, 3)
                V.tensor_copy(w1_p[:, :, 1, :], w1_r[:, :, :]).then_inc(s_w1_step, 1)
                dve.wait_ge(s_w1_step, 4)
                V.tensor_tensor(w1_p[:, :, 2, :], w1_r[:, :, :], w1_p[:, :, 1, :], ALU.subtract).then_inc(s_w1_step, 1)
                dve.wait_ge(s_w1_step, 5)
                for k in range(FB):
                    V.tensor_copy(w1_st[:, k, 0:9 * NQ].rearrange("p (i j q) -> p i j q", i=3, j=3),
                                  w1_p[:, k, None, :, 0:NQ].to_broadcast([P, 3, 3, NQ])).then_inc(s_w1_stack, 1)
                V.tensor_copy(w1_st[:, :, 9 * NQ:QK], w1_p[:, :, :, NQ]).then_inc(s_w1_stack, 1)

            def conv_project(b):
                dve.wait_ge(s_proj_ps, b + 1)
                v = conv_ps[:, 0:TB * (2 * D + C)].rearrange("p (t k) -> p t k", t=TB)
                V.tensor_tensor(FGs[:, b], v[:, :, 0:2 * D], bfg[:, None, :].to_broadcast([P, TB, 2 * D]), ALU.add).then_inc(s_fg, 1)

            def conv_stack(b):
                dve.wait_ge(s_stack_ps, b + 1)
                if b >= 2:
                    dve.wait_ge(s_cscore_ps, b - 1)
                V.tensor_copy(FGT[:, b % 2, :], b16(conv_ps)[:, 0:2 * N]).then_inc(s_stack, 1)

            def conv_scores(b):
                dve.wait_ge(s_cscore_ps, b + 1)
                V.tensor_reduce(nmx[:, b, :], conv_ps[:, :].rearrange("p (t n) -> p t n", t=TB), AX.X, ALU.max,
                                negate=True).then_inc(s_cmax, 1)

            def conv_turn(b):
                dve.wait_ge(s_ET_ps, b + 1)
                if b >= 2:
                    dve.wait_ge(s_O_ps, b - 1)
                V.tensor_copy(ETs[:, b % 2].rearrange("p t n -> p (t n)"), conv_ps[:, :]).then_inc(s_ET, 1)
                dve.wait_ge(s_cexp, b + 1)
                V.reciprocal(rden[:, b, :], den[:, b, :]).then_inc(s_crden, 1)
                dve.wait_ge(s_crden, b + 1)
                V.tensor_scalar(gden[:, b, :], rden[:, b, :], gam[:, 0:1], None, ALU.mult).then_inc(s_cgain, 1)

            def conv_output(b):
                dve.wait_ge(s_O_ps, b + 1)
                dve.wait_ge(s_xr, b + 1)
                dve.wait_ge(s_cgain, b + 1)
                for t in range(TB):
                    last = V.scalar_tensor_tensor(out=T0[:, b, t, :], in0=conv_ps[:, t * C:(t + 1) * C],
                                                  scalar=gden[:, b, t:t + 1], in1=XR[:, b, t, :], op0=ALU.mult, op1=ALU.add)
                last.then_inc(s_t0, 1)
                if b == 0:
                    stack_w1()

            def proj_norm(b):
                dve.wait_ge(s_t0, b + 1)
                norm_stats(b, T0[:, b], 0, s_y_stats, s_y_mv)

            def proj_angle(b):
                if b >= 2:
                    dve.wait_ge(s_y_bias, b - 1)
                norm_apply(b, Y[:, b % 2], T0[:, b], 0, s_y_rstd, s_y)

            def proj_reduce(b):
                dve.wait_ge(s_y_k, b + 1)
                if b >= 2:
                    dve.wait_ge(s_y_clamp, b - 1)
                A = ARG[:, b % 2]
                V.scalar_tensor_tensor(out=A[:, 3], in0=A[:, 2], scalar=-TWO_PI_HI, in1=A[:, 0],
                                       op0=ALU.mult, op1=ALU.add).then_inc(s_y_r1, 1)
                dve.wait_ge(s_y_r1, b + 1)
                V.scalar_tensor_tensor(out=A[:, 4], in0=A[:, 2], scalar=-TWO_PI_LO, in1=A[:, 3],
                                       op0=ALU.mult, op1=ALU.add).then_inc(s_y_r2, 1)
                dve.wait_ge(s_y_r2, b + 1)
                if b >= 2:
                    dve.wait_ge(s_y_cos, b - 1)
                V.tensor_scalar(A[:, 5], A[:, 4], PI_F32, -PI_F32, ALU.min, ALU.max).then_inc(s_y_clamp, 1)

            def proj_cos(b):
                dve.wait_ge(s_y_cos, b + 1)
                if b >= 2:
                    dve.wait_ge(s_p_aug, 2 * (b - 1))
                dve.wait_ge(s_const_set, 3)
                V.tensor_tensor_scan(SC[:, b % 2].rearrange("p t c -> p (t c)"), scanmask[:, :],
                                     CS[:, b % 2].rearrange("p t c -> p (t c)"), 1.0, ALU.max, ALU.mult).then_inc(s_scan, 1)

            def proj_split(b):
                dve.wait_ge(s_left_h, b + 1)
                V.tensor_tensor(LS[:, b % 2, :, :, 1].rearrange("p t h j d -> p (t h) j d"),
                                PA[:, b % 2, :, :, None, 0:DK].rearrange("p t h j d -> p (t h) j d").to_broadcast([P, TB * H, 2, DK]),
                                LS[:, b % 2, :, :, 0].rearrange("p t h j d -> p (t h) j d"), ALU.subtract).then_inc(s_left_l, 1)

            def attn_transpose(b):
                dve.wait_ge(s_LT_ps, b + 1)
                if b >= 1:
                    dve.wait_ge(s_score_ps, H * b)
                V.tensor_copy(LT[:, :, :].rearrange("p j n -> p (j n)"), b16(attn_ps, F16)).then_inc(s_LT, 1)
                dve.wait_ge(s_RT_ps, b + 1)
                dve.wait_ge(s_zeroed, 1)
                for i in range(2):
                    q = slice(64 * i, 64 * i + 64)
                    V.tensor_copy(RT[q, i, :, :].rearrange("p j n -> p (j n)"), b16(sc_ps[0], F16)[q, :]).then_inc(s_RT, 1)

            def attn_turn(b):
                dve.wait_ge(s_CTT_ps, b + 1)
                v = attn_ps[:, :].rearrange("p (k d) -> p k d", d=32)
                V.reciprocal(ard[:, :], v[:, :, DK]).then_inc(s_arden, 1)
                dve.wait_ge(s_arden, b + 1)
                V.tensor_tensor(CX[:, :, :].rearrange("p t (h d) -> p (t h) d", d=DK), v[:, :, 0:DK],
                                ard[:, :, None].to_broadcast([P, 2 * H, DK]), ALU.mult).then_inc(s_ctx, 1)

            def attn_combine(b):
                dve.wait_ge(s_comb_ps, b + 1)
                dve.wait_ge(s_y_bias, b + 1)
                V.tensor_tensor(Z[:, b % 2], tb_of(attn_ps[:, 0:TB * C]), YB[:, b % 4], ALU.add).then_inc(s_z, 1)

            def ffn_norm(b):
                dve.wait_ge(s_z, b + 1)
                norm_stats(b, Z[:, b % 2], 1, s_z_stats, s_z_mv)
                if b >= 2:
                    dve.wait_ge(s_x1_bias, b - 1)
                    dve.wait_ge(s_q_arg, b - 1)
                norm_affine(b, X1[:, b % 2], ZN[:, b % 2], Z[:, b % 2], 1, s_z_rstd, g1_b[:, :],
                            [be1_b[:, :]] * TB, s_z_n, s_x1)

            def ffn_angle(b):
                dve.wait_ge(s_q_k, b + 1)
                A = QA[:, b % 2]
                V.scalar_tensor_tensor(out=A[:, 3], in0=A[:, 2], scalar=-TWO_PI_HI, in1=A[:, 0],
                                       op0=ALU.mult, op1=ALU.add).then_inc(s_q_r1, 1)
                dve.wait_ge(s_q_r1, b + 1)
                V.scalar_tensor_tensor(out=A[:, 4], in0=A[:, 2], scalar=-TWO_PI_LO, in1=A[:, 3],
                                       op0=ALU.mult, op1=ALU.add).then_inc(s_q_r2, 1)
                dve.wait_ge(s_q_r2, b + 1)
                if b >= 2:
                    dve.wait_ge(s_q_cos, b - 1)
                V.tensor_scalar(A[:, 5], A[:, 4], PI_F32, -PI_F32, ALU.min, ALU.max).then_inc(s_q_clamp, 1)

            def ffn_transpose(b):
                dve.wait_ge(s_qT_ps, b + 1)
                if b >= 1:
                    dve.wait_ge(s_hid_ps, 2 * b)
                V.tensor_copy(QT[:, :], b16(ffn_ps)[0:QK, 0:N]).then_inc(s_qT, 1)

            def ffn_output(b):
                dve.wait_ge(s_ffn_ps, b + 1)
                dve.wait_ge(s_x1_bias, b + 1)
                V.tensor_tensor(Z2[:, b % 2], tb_of(ffn_ps[:, 0:TB * C]), X1B[:, b % 2], ALU.add).then_inc(s_z2, 1)

            def norm_second(b):
                dve.wait_ge(s_z2, b + 1)
                norm_stats(b, Z2[:, b % 2], 2, s_n_stats, s_n_mv)
                dve.wait_ge(s_t0_bias, b + 1)
                norm_affine(b, T1[:, b], NN[:, b % 2], Z2[:, b % 2], 2, s_n_rstd, g2_b[:, :],
                            [T0B[:, b % 2, t, :] for t in range(TB)], s_n_n, s_t1)

            def norm_third(b):
                dve.wait_ge(s_t1, b + 1)
                norm_stats(b, T1[:, b], 3, s_u_stats, s_u_mv)
                if b >= 2:
                    dve.wait_ge(s_xtT_ps, b - 1)
                norm_apply(b, XTK[:, b % 2], T1[:, b], 3, s_u_rstd, s_xt)

            def moe_select(b):
                dve.wait_ge(s_sel_e, b + 1)
                V.tensor_scalar(SE[:, b], SE[:, b], 1.0, None, ALU.add).then_inc(s_sel_1, 1)
                dve.wait_ge(s_sel_1, b + 1)
                V.reciprocal(SG[:, b, :, 0:E], SE[:, b]).then_inc(s_sel_s, 1)
                dve.wait_ge(s_sel_s, b + 1)
                for t in range(TB):
                    last = V.max(V8[:, b, t, :], SG[:, b, t, 0:E])
                last.then_inc(s_top8, 1)

            def moe_topk(b):
                dve.wait_ge(s_top8, b + 1)
                dve.wait_ge(s_const_set, 5)
                V.tensor_copy(R8[:, b, :, 0:2], V8[:, b, :, 0:2]).then_inc(s_top2, 1)
                dve.wait_ge(s_top2, b + 1)
                for t in range(TB):
                    last = V.match_replace(SR[:, b, t, :], R8[:, b, t, :], SG[:, b, t, :], 0.0)
                last.then_inc(s_rest, 1)

            def moe_spread(b):
                dve.wait_ge(s_wT_ps, b + 1)
                if b >= 2:
                    dve.wait_ge(s_moe_ps, 4 * (b - 1))
                V.tensor_copy(WT[:, b % 2, :], b16(moe_ps)[0:3 * E, 0:N]).then_inc(s_wT, 1)

            def moe_pair(b, q):
                n = 4 * b + q
                dve.wait_ge(s_relu, n + 1)
                dve.wait_ge(s_moe_ps, n + 1)
                if n >= 2:
                    dve.wait_ge(s_out_ps, n - 1)
                V.tensor_tensor(HWT[:, q % 2].rearrange("p i n -> p (i n)"), wide_ps[:, :], HR[:, q % 2, :], ALU.mult).then_inc(s_hw, 1)

            def moe_output(b):
                dve.wait_ge(s_out_ps, 4 * b + 4)
                if b >= 2:
                    dve.wait_ge(stored[b % 2], 16 * (b // 2))
                V.tensor_tensor(OB[:, b % 2], tb_of(moe_ps[:, 0:TB * C]), T1[:, b], ALU.add).then_inc(s_out_sb, 1)

            run_steps({
                "conv_project": conv_project, "conv_stack": conv_stack, "conv_scores": conv_scores,
                "conv_turn": conv_turn, "conv_output": conv_output, "proj_norm": proj_norm, "proj_angle": proj_angle,
                "proj_reduce": proj_reduce, "proj_cos": proj_cos, "proj_split": proj_split,
                "attn_transpose": attn_transpose, "attn_turn": attn_turn, "attn_combine": attn_combine,
                "ffn_norm": ffn_norm, "ffn_angle": ffn_angle, "ffn_transpose": ffn_transpose, "ffn_output": ffn_output,
                "norm_second": norm_second, "norm_third": norm_third, "moe_select": moe_select, "moe_topk": moe_topk,
                "moe_spread": moe_spread, "moe_pair": moe_pair, "moe_output": moe_output,
            })

        @block.gpsimd
        def _(pool):
            G = nc.gpsimd
            for m in (ident, identb, identh):
                G.memset(m[:, :], 0.0).then_inc(s_ident, 1)
            G.memset(spread[:, :, :], 0.0).then_inc(s_const_set, 1)
            pool.wait_ge(s_ident, 3)
            for m in (ident, identb, identh):
                G.affine_select(out=m[:, :], in_=m[:, :], compare_op=ALU.not_equal, fill=1.0, base=0,
                                pattern=[[-1, P]], channel_multiplier=1).then_inc(s_ident, 1)
            G.memset(scanmask[:, :], -2.0).then_inc(s_const_set, 1)
            pool.wait_ge(s_const_set, 2)
            G.memset(scanmask[:, :].rearrange("p (g d) -> p g d", d=DK)[:, :, 1:2], 1.0).then_inc(s_const_set, 1)
            G.memset(SG[:, :, :, E:E + 6], -1.0).then_inc(s_const_set, 1)
            G.memset(R8[:, :, :, 2:8], -1.0).then_inc(s_const_set, 1)
            G.memset(minushalf[:, :], -0.5).then_inc(s_ones_set, 1)
            G.memset(PA[:, :, :, :, DK:32], 1.0).then_inc(s_ones_set, 1)
            G.memset(QS[:, :, :, 9 * NQ:QK], 1.0).then_inc(s_ones_set, 1)
            G.memset(RT[:, :, :, :], 0.0).then_inc(s_zeroed, 1)
            pool.wait_ge(s_zeroed, 1)
            for i in range(3):
                if i:
                    pool.wait_ge(s_spread_set, i)
                v = spread[i * E:(i + 1) * E, :, :].rearrange("p k (e h) -> p k e h", e=EPB)
                G.affine_select(out=v, in_=v, compare_op=ALU.not_equal, fill=1.0, base=0,
                                pattern=[[-EPB, EB], [-1, EPB], [0, HE]], channel_multiplier=1).then_inc(s_spread_set, 1)
            pool.wait_ge(s_ones_set, 3)
            pool.wait_ge(s_spread_set, 3)
            pool.wait_ge(s_rc, 1)

            def rsqrt(b, which, mvs, vs, rs):
                pool.wait_ge(mvs, b + 1)
                G.tensor_scalar(var[:, which, b, :], mv[:, which, b, :, 1], EPS, 1.0, ALU.add, ALU.mult).then_inc(vs, 1)
                pool.wait_ge(vs, b + 1)
                G.tensor_tensor(rstd[:, which, b, :], var[:, which, b, :], minushalf[:, :], ALU.pow).then_inc(rs, 1)

            def reduce_angle(b, A, a, k1, k):
                pool.wait_ge(a, b + 1)
                G.tensor_scalar(A[:, 1], A[:, 0], 0.5 / math.pi, ROUND, ALU.mult, ALU.add).then_inc(k1, 1)
                pool.wait_ge(k1, b + 1)
                G.tensor_scalar(A[:, 2], A[:, 1], -ROUND, 1.0, ALU.add, ALU.mult).then_inc(k, 1)

            def conv_transpose(b):
                pool.wait_ge(x_in[b], 16)
                G.tensor_tensor(XR[:, b], X[:, b], rc[:, None, :].to_broadcast([P, TB, C]), ALU.add).then_inc(s_xr, 1)

            def conv_project(b):
                pool.wait_ge(s_fg, b + 1)
                if b >= 2:
                    pool.wait_ge(s_stack_ps, b - 1)
                st_f = FGp[:, b % 2, :, 0].rearrange("p t (i j) d -> p t i j d", i=3)
                st_g = FGp[:, b % 2, :, 1].rearrange("p t (i j) d -> p t i j d", i=3)

                def three(src, side):
                    return src[:, :, None, side * D:(side + 1) * D].to_broadcast([P, TB, 3, D])
                G.tensor_copy(st_f[:, :, 0], three(FGs[:, b], 0)).then_inc(s_fg_h, 1)
                G.tensor_copy(st_g[:, :, :, 0], three(FGs[:, b], 1)).then_inc(s_fg_h, 1)
                pool.wait_ge(s_fg_h, 2 * b + 2)
                G.tensor_tensor(FGr[:, b].rearrange("p t (s d) -> p t s d", s=2), FGs[:, b].rearrange("p t (s d) -> p t s d", s=2),
                                FGp[:, b % 2, :, :, 0], ALU.subtract).then_inc(s_fg_r, 1)
                pool.wait_ge(s_fg_r, b + 1)
                G.tensor_copy(st_f[:, :, 1], three(FGr[:, b], 0)).then_inc(s_fg_m, 1)
                G.tensor_copy(st_g[:, :, :, 1], three(FGr[:, b], 1)).then_inc(s_fg_m, 1)
                pool.wait_ge(s_fg_m, 2 * b + 2)
                G.tensor_tensor(st_f[:, :, 2], three(FGr[:, b], 0), st_f[:, :, 1], ALU.subtract).then_inc(s_fg_l, 1)
                G.tensor_tensor(st_g[:, :, :, 2], three(FGr[:, b], 1), st_g[:, :, :, 1], ALU.subtract).then_inc(s_fg_l, 1)

            def proj_norm(b):
                rsqrt(b, 0, s_y_mv, s_y_var, s_y_rstd)

            def proj_angle(b):
                pool.wait_ge(s_y, b + 1)
                if b == 0:
                    pool.wait_ge(s_theta2, 1)
                    pool.wait_ge(w2_in, W2_LOADED)
                if b >= 2:
                    pool.wait_ge(s_y_r2, b - 1)
                G.tensor_tensor(ARG[:, b % 2, 0].rearrange("p t (h d) -> p (t h) d", d=DK),
                                Y[:, b % 2].rearrange("p t (h d) -> p (t h) d", d=DK),
                                theta2[:, None, :].to_broadcast([P, TB * H, DK]), ALU.add).then_inc(s_y_arg, 1)
                reduce_angle(b, ARG[:, b % 2], s_y_arg, s_y_k1, s_y_k)
                if b >= 4:
                    pool.wait_ge(s_z, b - 3)
                G.tensor_tensor(YB[:, b % 4], Y[:, b % 2], bc_b[:, None, :].to_broadcast([P, TB, C]), ALU.add).then_inc(s_y_bias, 1)

            def proj_split(b):
                pool.wait_ge(s_scan, b + 1)
                if b >= 2:
                    pool.wait_ge(s_ctx_ps, 2 * (b - 1))
                    pool.wait_ge(s_RT_ps, b - 1)
                q = SC[:, b % 2].rearrange("p t (h d) -> p (t h) d", d=DK)
                c = CS[:, b % 2].rearrange("p t (h d) -> p (t h) d", d=DK)
                a = PA[:, b % 2].rearrange("p t h d -> p (t h) d")
                G.tensor_tensor(a[:, :, 1:DK], q[:, :, 1:DK], c[:, :, 0:1].to_broadcast([P, TB * H, DK - 1]), ALU.mult).then_inc(s_p_aug, 1)
                G.tensor_copy(a[:, :, 0:1], q[:, :, DK - 1:DK]).then_inc(s_p_aug, 1)
                l = LS[:, b % 2].rearrange("p t h i j d -> p (t h) (i j d)").bitcast(U32).rearrange("p k (i j d) -> p k i j d", i=2, j=2)
                r = RS[:, b % 2].rearrange("p t h i j d -> p (t h) (i j d)").bitcast(U32).rearrange("p k (i j d) -> p k i j d", i=2, j=2)
                pool.wait_ge(s_left_h, b + 1)
                G.tensor_copy(r[:, :, :, 0], l[:, :, 0]).then_inc(s_right, 1)
                pool.wait_ge(s_left_l, b + 1)
                G.tensor_copy(r[:, :, :, 1], l[:, :, 1]).then_inc(s_right, 1)

            def ffn_norm(b):
                rsqrt(b, 1, s_z_mv, s_z_var, s_z_rstd)
                pool.wait_ge(s_x1, b + 1)
                if b >= 2:
                    pool.wait_ge(s_q_r2, b - 1)
                G.tensor_scalar(QA[:, b % 2, 0], X1[:, b % 2, :, 0:NQ], math.pi / 2, 1.0, ALU.add, ALU.mult).then_inc(s_q_arg, 1)
                reduce_angle(b, QA[:, b % 2], s_q_arg, s_q_k1, s_q_k)
                if b >= 2:
                    pool.wait_ge(s_z2, b - 1)
                G.tensor_tensor(X1B[:, b % 2], X1[:, b % 2], b2_b[:, None, :].to_broadcast([P, TB, C]), ALU.add).then_inc(s_x1_bias, 1)

            def ffn_cos(b):
                v = QS[:, b, :, 0:9 * NQ].rearrange("p t (i j q) -> p t i j q", i=3, j=3)

                def three(src):
                    return src[:, :, None, :].to_broadcast([P, TB, 3, NQ])
                pool.wait_ge(s_q_cos, b + 1)
                G.tensor_copy(v[:, :, 0], three(QC[:, b])).then_inc(s_q_h, 1)
                pool.wait_ge(s_q_h, b + 1)
                G.tensor_tensor(QR[:, b], QC[:, b], v[:, :, 0, 0], ALU.subtract).then_inc(s_q_r, 1)
                pool.wait_ge(s_q_r, b + 1)
                G.tensor_copy(v[:, :, 1], three(QR[:, b])).then_inc(s_q_m, 1)
                pool.wait_ge(s_q_m, b + 1)
                G.tensor_tensor(v[:, :, 2], three(QR[:, b]), v[:, :, 1], ALU.subtract).then_inc(s_q_l, 1)

            def norm_second(b):
                if b >= 2:
                    pool.wait_ge(s_t1, b - 1)
                G.tensor_tensor(T0B[:, b % 2], T0[:, b], be2_b[:, None, :].to_broadcast([P, TB, C]), ALU.add).then_inc(s_t0_bias, 1)
                rsqrt(b, 2, s_n_mv, s_n_var, s_n_rstd)

            def norm_third(b):
                rsqrt(b, 3, s_u_mv, s_u_var, s_u_rstd)

            def moe_topk(b):
                pool.wait_ge(s_rest, b + 1)
                G.tensor_tensor(W[:, b], SG[:, b, :, 0:E], SR[:, b, :, 0:E], ALU.subtract).then_inc(s_w, 1)
                pool.wait_ge(s_w, b + 1)
                G.tensor_copy(WP[:, b, :, 0, :], W[:, b]).then_inc(s_w_h, 1)
                pool.wait_ge(s_w_h, b + 1)
                G.tensor_tensor(WR[:, b], W[:, b], WP[:, b, :, 0, :], ALU.subtract).then_inc(s_w_r, 1)
                pool.wait_ge(s_w_r, b + 1)
                G.tensor_copy(WP[:, b, :, 1, :], WR[:, b]).then_inc(s_w_m, 1)
                pool.wait_ge(s_w_m, b + 1)
                G.tensor_tensor(WP[:, b, :, 2, :], WR[:, b], WP[:, b, :, 1, :], ALU.subtract).then_inc(s_w_l, 1)

            run_steps({
                "conv_transpose": conv_transpose, "conv_project": conv_project, "proj_norm": proj_norm,
                "proj_angle": proj_angle, "proj_split": proj_split,
                "ffn_norm": ffn_norm, "ffn_cos": ffn_cos,
                "norm_second": norm_second, "norm_third": norm_third, "moe_topk": moe_topk,
            })


_INS = ["x", "L0_conv_Wf", "L0_conv_bf", "L0_conv_Wg", "L0_conv_bg", "L0_conv_Wh", "L0_conv_bh", "L0_conv_Wv",
        "L0_conv_bv", "L0_conv_gamma", "L1_attn_theta_attn", "L1_attn_phi_ffn", "L1_attn_W_comb", "L1_attn_b_comb",
        "L1_attn_W1", "L1_attn_b1", "L1_attn_W2", "L1_attn_b2", "L1_attn_ln1_g", "L1_attn_ln1_b", "L1_attn_ln2_g",
        "L1_attn_ln2_b", "L1_ffn_expert_sel", "L1_ffn_keys", "L1_ffn_values"]


def kernel(**inputs):
    import numpy as _np
    import concourse.bacc as _bacc
    from concourse import mybir as _mybir
    from concourse.bass_utils import run_bass_kernel_spmd as _run

    nc = _bacc.Bacc("TRN2", target_bir_lowering=False, num_devices=1)
    arrays, args = {}, []
    for name in _INS:
        a = _np.ascontiguousarray(inputs[name])
        arrays[f"in_{name}"] = a
        args.append(nc.dram_tensor(f"in_{name}", a.shape, _mybir.dt.from_np(a.dtype), kind="ExternalInput").ap())
    x = inputs["x"]
    args.append(nc.dram_tensor("out_0", x.shape, _mybir.dt.from_np(_np.dtype("float32")), kind="ExternalOutput").ap())
    build(nc, *args)
    r = _run(nc, [arrays], core_ids=[0])
    return r.results[0]["out_0"]
```

```python
from contextlib import ExitStack
import math

import concourse.bass as bass
from concourse import mybir

F32 = mybir.dt.float32
BF16 = mybir.dt.bfloat16
F16 = mybir.dt.float16
U32 = mybir.dt.uint32
ALU = mybir.AluOpType
ACT = mybir.ActivationFunctionType
AX = mybir.AxisListType

P = 128
ROUND = 1.5 * 2.0 ** 23
TWO_PI_HI = 6.28125
TWO_PI_LO = 2.0 * math.pi - TWO_PI_HI
PI_F32 = 3.1415925
EPS = 1e-5
W_SCALE = 4096.0

START = {
    "conv_transpose": 0.000, "conv_project": 0.131, "conv_stack": 0.478, "conv_scores": 0.664, "conv_turn": 0.991,
    "conv_output": 1.190,
    "proj_norm": 0.000, "proj_angle": 0.375, "proj_reduce": 0.557, "proj_cos": 0.794, "proj_split": 1.014,
    "attn_transpose": 0.000, "attn_scores0": 0.123, "attn_scores1": 0.129, "attn_scores2": 0.267,
    "attn_scores3": 0.295, "attn_context0": 0.465, "attn_scores4": 0.494, "attn_scores5": 0.508,
    "attn_scores6": 0.552, "attn_scores7": 0.608, "attn_context1": 0.762, "attn_turn": 0.852, "attn_back": 1.085,
    "attn_combine": 1.209,
    "ffn_norm": 0.000, "ffn_angle": 0.372, "ffn_cos": 0.622, "ffn_transpose": 0.911, "ffn_hidden0": 1.301,
    "ffn_hidden1": 1.545, "ffn_output": 1.730,
    "norm_second": 0.000, "norm_third": 0.386,
    "moe_transpose": 0.000, "moe_select": 0.095, "moe_topk": 0.125, "moe_spread": 0.395, "moe_pair0": 0.535,
    "moe_pair1": 0.716, "moe_pair2": 0.998, "moe_pair3": 1.157, "moe_output": 1.189,
}


CHAIN = {
    "conv": (0.000, 4.654, 5.883, 7.128, 8.599, 9.969, 11.330, 12.652),
    "proj": (4.213, 6.104, 7.449, 8.826, 10.191, 11.562, 12.928, 14.505),
    "attn": (5.828, 7.430, 8.902, 10.276, 11.607, 12.925, 14.284, 15.872),
    "ffn": (7.444, 8.943, 10.284, 11.705, 13.063, 14.512, 16.131, 17.455),
    "norm": (9.557, 10.883, 12.224, 14.018, 15.617, 16.569, 18.277, 19.630),
    "moe": (10.535, 11.888, 13.236, 14.828, 16.048, 17.547, 18.900, 20.600),
}


def build(nc, x, Wf, bf, Wg, bg, Wh, bh, Wv, bv, gamma, theta, phi, W_comb, b_comb, W1, b1, W2, b2,
          ln1_g, ln1_b, ln2_g, ln2_b, expert_sel, keys, values, out):
    NB, IH, IW, C = x.shape
    N = IH * IW
    TB = N // P
    D = Wf.shape[1]
    DK = theta.shape[0]
    H = C // DK
    FF, NQ = W1.shape
    FB = FF // P
    E, _, HE = keys.shape
    EB = E * HE // P
    EPB = P // HE
    assert C == P and D == DK == 16 and TB == 2 and 2 * N == 512 and E * 3 == 96
    xv = x.rearrange("b h w c -> b (h w) c").rearrange("b (t p) c -> b p t c", p=P)
    ov = out.rearrange("b h w c -> b (h w) c").rearrange("b (t p) c -> b p t c", p=P)

    with ExitStack() as es:
        def sb(name, shape, dt=F32):
            return es.enter_context(nc.sbuf_tensor(name, shape, dt))

        def ps(name, dt=F32):
            return es.enter_context(nc.psum_tensor(name, [P, 2048 // (4 if dt == F32 else 2)], dt))

        def sem(name):
            return es.enter_context(nc.semaphore(name))

        s_ident = sem("s_ident")
        s_spread_set = sem("s_spread_set")
        s_zeroed = sem("s_zeroed")
        s_ones_set = sem("s_ones_set")
        s_const_set = sem("s_const_set")
        s_wproj_sb = sem("s_wproj_sb")
        s_whT_ps = sem("s_whT_ps")
        s_whT = sem("s_whT")
        s_wv_ps = sem("s_wv_ps")
        s_rc_ps = sem("s_rc_ps")
        s_rc = sem("s_rc")
        s_bh_row = sem("s_bh_row")
        s_b1T_ps = sem("s_b1T_ps")
        s_b1 = sem("s_b1")
        s_wcT_ps = sem("s_wcT_ps")
        s_wcT = sem("s_wcT")
        s_w2T_ps = sem("s_w2T_ps")
        s_w2T = sem("s_w2T")
        s_selT_ps = sem("s_selT_ps")
        s_selT = sem("s_selT")
        s_phi_step = sem("s_phi_step")
        s_phi_clamp = sem("s_phi_clamp")
        s_phi_cos = sem("s_phi_cos")
        s_w1_step = sem("s_w1_step")
        s_w1_stack = sem("s_w1_stack")
        s_w1T_ps = sem("s_w1T_ps")
        s_w1T = sem("s_w1T")
        s_theta2 = sem("s_theta2")
        s_xT_ps = sem("s_xT_ps")
        s_xT = sem("s_xT")
        s_proj_ps = sem("s_proj_ps")
        s_fg = sem("s_fg")
        s_hW = sem("s_hW")
        s_fg_h = sem("s_fg_h")
        s_fg_r = sem("s_fg_r")
        s_fg_m = sem("s_fg_m")
        s_fg_l = sem("s_fg_l")
        s_stack_ps = sem("s_stack_ps")
        s_stack = sem("s_stack")
        s_cscore_ps = sem("s_cscore_ps")
        s_cmax = sem("s_cmax")
        s_cexp = sem("s_cexp")
        s_ET_ps = sem("s_ET_ps")
        s_ET = sem("s_ET")
        s_O_ps = sem("s_O_ps")
        s_xr = sem("s_xr")
        s_crden = sem("s_crden")
        s_cgain = sem("s_cgain")
        s_t0 = sem("s_t0")
        s_y_stats = sem("s_y_stats")
        s_y_mv = sem("s_y_mv")
        s_y_var = sem("s_y_var")
        s_y_rstd = sem("s_y_rstd")
        s_y = sem("s_y")
        s_y_arg = sem("s_y_arg")
        s_y_k1 = sem("s_y_k1")
        s_y_k = sem("s_y_k")
        s_y_r1 = sem("s_y_r1")
        s_y_r2 = sem("s_y_r2")
        s_y_clamp = sem("s_y_clamp")
        s_y_cos = sem("s_y_cos")
        s_y_bias = sem("s_y_bias")
        s_scan = sem("s_scan")
        s_p_aug = sem("s_p_aug")
        s_left_h = sem("s_left_h")
        s_left_l = sem("s_left_l")
        s_right = sem("s_right")
        s_LT_ps = sem("s_LT_ps")
        s_LT = sem("s_LT")
        s_RT_ps = sem("s_RT_ps")
        s_RT = sem("s_RT")
        s_score_ps = sem("s_score_ps")
        s_prob = sem("s_prob")
        s_ctx_ps = sem("s_ctx_ps")
        s_CT = sem("s_CT")
        s_CTT_ps = sem("s_CTT_ps")
        s_arden = sem("s_arden")
        s_ctx = sem("s_ctx")
        s_ctxT_ps = sem("s_ctxT_ps")
        s_ctxT = sem("s_ctxT")
        s_comb_ps = sem("s_comb_ps")
        s_z = sem("s_z")
        s_z_stats = sem("s_z_stats")
        s_z_mv = sem("s_z_mv")
        s_z_var = sem("s_z_var")
        s_z_rstd = sem("s_z_rstd")
        s_z_n = sem("s_z_n")
        s_x1 = sem("s_x1")
        s_x1_bias = sem("s_x1_bias")
        s_q_arg = sem("s_q_arg")
        s_q_k1 = sem("s_q_k1")
        s_q_k = sem("s_q_k")
        s_q_r1 = sem("s_q_r1")
        s_q_r2 = sem("s_q_r2")
        s_q_clamp = sem("s_q_clamp")
        s_q_cos = sem("s_q_cos")
        s_q_h = sem("s_q_h")
        s_q_r = sem("s_q_r")
        s_q_m = sem("s_q_m")
        s_q_l = sem("s_q_l")
        s_qT_ps = sem("s_qT_ps")
        s_qT = sem("s_qT")
        s_hid_ps = sem("s_hid_ps")
        s_hid = sem("s_hid")
        s_ffn_ps = sem("s_ffn_ps")
        s_z2 = sem("s_z2")
        s_n_stats = sem("s_n_stats")
        s_n_mv = sem("s_n_mv")
        s_n_var = sem("s_n_var")
        s_n_rstd = sem("s_n_rstd")
        s_n_n = sem("s_n_n")
        s_t0_bias = sem("s_t0_bias")
        s_t1 = sem("s_t1")
        s_u_stats = sem("s_u_stats")
        s_u_mv = sem("s_u_mv")
        s_u_var = sem("s_u_var")
        s_u_rstd = sem("s_u_rstd")
        s_xt = sem("s_xt")
        s_xtT_ps = sem("s_xtT_ps")
        s_xtT = sem("s_xtT")
        s_sel_ps = sem("s_sel_ps")
        s_sel_e = sem("s_sel_e")
        s_sel_1 = sem("s_sel_1")
        s_sel_s = sem("s_sel_s")
        s_top8 = sem("s_top8")
        s_top2 = sem("s_top2")
        s_rest = sem("s_rest")
        s_w = sem("s_w")
        s_w_h = sem("s_w_h")
        s_w_l = sem("s_w_l")
        s_wT_ps = sem("s_wT_ps")
        s_wT = sem("s_wT")
        s_moe_ps = sem("s_moe_ps")
        s_relu = sem("s_relu")
        s_hw = sem("s_hw")
        s_out_ps = sem("s_out_ps")
        s_out_sb = sem("s_out_sb")
        x_in = [sem(f"x_in{b}") for b in range(NB)]
        stored = [sem(f"stored{i}") for i in range(2)]
        w0_in = sem("w0_in")
        w_in = sem("w_in")
        w1_in = sem("w1_in")
        w2_in = sem("w2_in")
        w3_in = sem("w3_in")

        ident = sb("ident", [P, P])
        identb = sb("identb", [P, P], BF16)
        identh = sb("identh", [P, P], F16)
        spread = sb("spread", [3 * E, EB, P], F16)
        scanmask = sb("scanmask", [P, TB * C])
        minushalf = sb("minushalf", [P, TB])
        wproj = sb("wproj", [P, 2 * D + C])
        wh_sb = sb("wh_sb", [P, D])
        whT_sb = sb("whT_sb", [D, P])
        wv_sb = sb("wv_sb", [D, C])
        bh_sb = sb("bh_sb", [D, 1])
        bh_row = sb("bh_row", [D, P])
        bfg = sb("bfg", [P, 2 * D])
        bv_b = sb("bv_b", [P, C])
        gam = sb("gam", [P, 1])
        rc = sb("rc", [P, C])
        theta_b = sb("theta_b", [P, DK])
        theta2 = sb("theta2", [P, DK])
        phi_b = sb("phi_b", [P, NQ])
        phi_t = sb("phi_t", [P, 6, NQ])
        wc_sb = sb("wc_sb", [P, C])
        wcT_sb = sb("wcT_sb", [P, C])
        w2_sb = sb("w2_sb", [P, FF])
        w2T_sb = sb("w2T_sb", [P, FB, C])
        w1_sb = sb("w1_sb", [P, FB, NQ])
        b1_sb = sb("b1_sb", [FB, P])
        w1_c = sb("w1_c", [P, FB, NQ + 1])
        w1_r = sb("w1_r", [P, FB, NQ + 1])
        w1_p = sb("w1_p", [P, FB, 3, NQ + 1], BF16)
        QK = 9 * NQ + 3
        w1_st = sb("w1_st", [P, FB, QK], BF16)
        w1T_sb = sb("w1T_sb", [QK, FF], BF16)
        bc_b = sb("bc_b", [P, C])
        b2_b = sb("b2_b", [P, C])
        g1_b = sb("g1_b", [P, C])
        be1_b = sb("be1_b", [P, C])
        g2_b = sb("g2_b", [P, C])
        be2_b = sb("be2_b", [P, C])
        sel_sb = sb("sel_sb", [E, C])
        selT_sb = sb("selT_sb", [P, E])
        keys_sb = sb("keys_sb", [P, E, HE])
        val_sb = sb("val_sb", [P, EB, C])

        X = sb("X", [P, NB, TB, C])
        XR = sb("XR", [P, NB, TB, C])
        XT = sb("XT", [P, 2, N])
        HW = sb("HW", [P, 2, TB, C])
        FGs = sb("FGs", [P, NB, TB, 2 * D])
        FGr = sb("FGr", [P, NB, TB, 2 * D])
        FGp = sb("FGp", [P, 2, TB, 2, 9, D], BF16)
        FGT = sb("FGT", [P, 2, 2 * N], BF16)
        nmx = sb("nmx", [P, NB, TB])
        den = sb("den", [P, NB, TB])
        rden = sb("rden", [P, NB, TB])
        gden = sb("gden", [P, NB, TB])
        EA = sb("EA", [P, 2, TB, N])
        ETs = sb("ETs", [P, 2, TB, N])
        T0 = sb("T0", [P, NB, TB, C])
        T1 = sb("T1", [P, NB, TB, C])
        st = sb("st", [P, 4, NB, TB, 6])
        mv = sb("mv", [P, 4, NB, TB, 2])
        var = sb("var", [P, 4, NB, TB])
        rstd = sb("rstd", [P, 4, NB, TB])
        Y = sb("Y", [P, 2, TB, C])
        YB = sb("YB", [P, 4, TB, C])
        ARG = sb("ARG", [P, 2, 6, TB, C])
        CS = sb("CS", [P, 2, TB, C])
        SC = sb("SC", [P, 2, TB, C])
        PA = sb("PA", [P, 2, TB, H, 32])
        LS = sb("LS", [P, 2, TB, H, 2, 2, DK], F16)
        RS = sb("RS", [P, 2, TB, H, 2, 2, DK], F16)
        LT = sb("LT", [P, H // 2, N], F16)
        RT = sb("RT", [P, 2, H // 2, N], F16)
        EB_ = sb("EB_", [P, H, TB, N])
        CT = sb("CT", [P, 2 * N])
        ard = sb("ard", [P, 2 * H])
        CX = sb("CX", [P, TB, C])
        CXT = sb("CXT", [P, N])
        Z = sb("Z", [P, 2, TB, C])
        ZN = sb("ZN", [P, 2, TB, C])
        X1 = sb("X1", [P, 2, TB, C])
        X1B = sb("X1B", [P, 2, TB, C])
        QA = sb("QA", [P, 2, 6, TB, NQ])
        QC = sb("QC", [P, NB, TB, NQ])
        QR = sb("QR", [P, NB, TB, NQ])
        QS = sb("QS", [P, NB, TB, QK], BF16)
        QT = sb("QT", [QK, N], BF16)
        HID = sb("HID", [P, FB, N])
        Z2 = sb("Z2", [P, 2, TB, C])
        NN = sb("NN", [P, 2, TB, C])
        T0B = sb("T0B", [P, 2, TB, C])
        XTK = sb("XTK", [P, 2, TB, C])
        XTT = sb("XTT", [P, 2, N])
        SE = sb("SE", [P, NB, TB, E])
        SG = sb("SG", [P, NB, TB, E + 6])
        V8 = sb("V8", [P, NB, TB, 8])
        R8 = sb("R8", [P, NB, TB, 8])
        SR = sb("SR", [P, NB, TB, E + 6])
        W = sb("W", [P, NB, TB, E])
        WP = sb("WP", [P, NB, TB, 3, E], F16)
        WT = sb("WT", [3 * E, 2, N], F16)
        HR = sb("HR", [P, 4, N])
        HWT = sb("HWT", [P, 4, N])
        OB = sb("OB", [P, 2, TB, C])

        conv_ps = ps("conv_ps")
        attn_ps = ps("attn_ps")
        sc_ps = [ps("sc0_ps"), ps("sc1_ps")]
        ffn_ps = ps("ffn_ps")
        hidden_ps = [ps("hidden0_ps"), ps("hidden1_ps")]
        moe_ps = ps("moe_ps")

        def b16(bank, dt=BF16):
            return bank[:, :].bitcast(dt)

        def tb_of(ap):
            return ap.rearrange("p (t c) -> p t c", t=TB)

        block = es.enter_context(nc.Block())

        @block.sync
        def _(sp):
            sp.dma_start(wh_sb[:, :], Wh).then_inc(w0_in, 16)
            sp.dma_start(X[:, 0], xv[0]).then_inc(x_in[0], 16)
            sp.dma_start(wproj[:, 0:D], Wf).then_inc(w_in, 16)
            sp.dma_start(bfg[:, 0:D], bf.partition_broadcast(P)).then_inc(w_in, 16)
            sp.dma_start(gam[:, :], gamma.partition_broadcast(P)).then_inc(w_in, 16)
            for dst, src in ((phi_b[:, :], phi.partition_broadcast(P)),
                             (w1_sb[:, :, :], W1.rearrange("(k p) q -> p k q", p=P)),
                             (b1_sb[:, :], b1.rearrange("(k p) -> k p", p=P))):
                sp.dma_start(dst, src).then_inc(w1_in, 16)
            sp.dma_start(X[:, 1], xv[1]).then_inc(x_in[1], 16)
            for dst, src in ((wc_sb[:, :], W_comb), (w2_sb[:, :], W2), (sel_sb[:, :], expert_sel),
                             (theta_b[:, :], theta.partition_broadcast(P))):
                sp.dma_start(dst, src).then_inc(w2_in, 16)
            sp.dma_start(X[:, 2], xv[2]).then_inc(x_in[2], 16)
            for dst, src in ((bc_b, b_comb), (g1_b, ln1_g), (be1_b, ln1_b), (b2_b, b2), (g2_b, ln2_g), (be2_b, ln2_b)):
                sp.dma_start(dst[:, :], src.partition_broadcast(P)).then_inc(w2_in, 16)
            for b in range(3, NB):
                sp.dma_start(X[:, b], xv[b]).then_inc(x_in[b], 16)
            sp.dma_start(keys_sb[:, :, :], keys.rearrange("e d h -> d e h")).then_inc(w3_in, 16)
            sp.dma_start(val_sb[:, :, :], values.rearrange("(k e) h v -> (e h) k v", k=EB)).then_inc(w3_in, 16)
            for b in range(NB):
                sp.wait_ge(s_out_sb, b + 1)
                sp.dma_start(ov[b], OB[:, b % 2]).then_inc(stored[b % 2], 16)
            for i in range(2):
                sp.wait_ge(stored[i], 16 * (NB // 2))

        W0_LOADED = 16 * 3
        W_LOADED = 16 * 6
        W1_LOADED = 16 * 3
        W2_LOADED = 16 * 10
        W3_LOADED = 16 * 2

        def run_steps(steps):
            for _, b, name in sorted((at + CHAIN[name.split("_")[0]][b], b, name)
                                     for name, at in START.items() for b in range(NB)):
                step = name.rstrip("0123456789")
                if name in steps:
                    steps[name](b)
                elif step in steps:
                    steps[step](b, int(name[len(step):]))

        @block.tensor
        def _(pe):
            mm, tr = nc.tensor.matmul, nc.tensor.transpose
            pe.wait_ge(w0_in, W0_LOADED)
            pe.wait_ge(s_ident, 4)
            tr(hidden_ps[0][0:D, 0:P], wh_sb[:, :], ident[:, :]).then_inc(s_whT_ps, 1)
            pe.wait_ge(s_bh_row, 1)
            mm(sc_ps[0][:, 0:C], bh_row[:, :], wv_sb[:, :], start=True, stop=True).then_inc(s_rc_ps, 1)
            pe.wait_ge(s_whT, 1)
            mm(hidden_ps[1][:, 0:C], whT_sb[:, :], wv_sb[:, :], start=True, stop=True).then_inc(s_wv_ps, 1)

            def turn_weights():
                pe.wait_ge(w2_in, W2_LOADED)
                tr(attn_ps[:, 0:P], wc_sb[:, :], ident[:, :]).then_inc(s_wcT_ps, 1)
                for k in range(FB):
                    last = tr(ffn_ps[:, k * P:(k + 1) * P], w2_sb[:, k * P:(k + 1) * P], ident[:, :])
                last.then_inc(s_w2T_ps, 1)
                tr(moe_ps[:, 0:E], sel_sb[:, :], ident[0:E, 0:E]).then_inc(s_selT_ps, 1)
                pe.wait_ge(w1_in, W1_LOADED)
                tr(hidden_ps[1][:, 0:FB], b1_sb[:, :], ident[0:FB, 0:FB]).then_inc(s_b1T_ps, 1)

            def turn_w1():
                pe.wait_ge(s_w1_stack, 5)
                for k in range(FB):
                    last = tr(b16(hidden_ps[0])[0:QK, k * P:(k + 1) * P], w1_st[:, k, :], identb[:, :])
                last.then_inc(s_w1T_ps, 1)

            def conv_transpose(b):
                pe.wait_ge(x_in[b], 16)
                if b:
                    pe.wait_ge(s_t0, b)
                for t in range(TB):
                    last = tr(conv_ps[:, t * P:(t + 1) * P], X[:, b, t, :], ident[:, :])
                last.then_inc(s_xT_ps, 1)

            def conv_project(b):
                pe.wait_ge(s_xT, b + 1)
                if b == 0:
                    pe.wait_ge(w_in, W_LOADED)
                    pe.wait_ge(s_wproj_sb, 1)
                for t in range(TB):
                    last = mm(conv_ps[:, t * (2 * D + C):(t + 1) * (2 * D + C)], XT[:, b % 2, t * P:(t + 1) * P],
                              wproj[:, :], start=True, stop=True)
                last.then_inc(s_proj_ps, 1)

            def conv_stack(b):
                pe.wait_ge(s_hW, b + 1)
                pe.wait_ge(s_fg_l, 2 * b + 2)
                if b == 0:
                    pe.wait_ge(s_ident, 6)
                for t in range(TB):
                    for side in range(2):
                        last = tr(b16(conv_ps)[:, side * N + t * P:side * N + (t + 1) * P],
                                  FGp[:, b % 2, t, side, 0:8, :].rearrange("p i d -> p (i d)"), identb[:, :])
                last.then_inc(s_stack_ps, 1)

            def conv_scores(b):
                pe.wait_ge(s_stack, b + 1)
                for t in range(TB):
                    last = mm(conv_ps[:, t * N:(t + 1) * N], FGT[:, b % 2, t * P:(t + 1) * P], FGT[:, b % 2, N:2 * N],
                              start=True, stop=True)
                last.then_inc(s_cscore_ps, 1)

            def conv_turn(b):
                pe.wait_ge(s_cexp, b + 1)
                for m in range(TB):
                    for t in range(TB):
                        last = tr(conv_ps[:, m * N + t * P:m * N + (t + 1) * P], EA[:, b % 2, t, m * P:(m + 1) * P],
                                  ident[:, :])
                last.then_inc(s_ET_ps, 1)

            def conv_output(b):
                pe.wait_ge(s_ET, b + 1)
                for t in range(TB):
                    for m in range(TB):
                        last = mm(conv_ps[:, t * C:(t + 1) * C], ETs[:, b % 2, m, t * P:(t + 1) * P],
                                  HW[:, b % 2, m, :], start=(m == 0), stop=(m == TB - 1))
                last.then_inc(s_O_ps, 1)
                if b == 0:
                    turn_weights()

            def attn_transpose(b):
                if b == 0:
                    pe.wait_ge(s_wcT, 1)
                    pe.wait_ge(s_rc, 1)
                if b:
                    pe.wait_ge(s_z, b)
                pe.wait_ge(s_left_l, b + 1)
                pe.wait_ge(s_right, 2 * b + 2)
                for j in range(H // 2):
                    for t in range(TB):
                        last = tr(b16(attn_ps, F16)[:, j * N + t * P:j * N + (t + 1) * P],
                                  LS[:, b % 2, t, 2 * j:2 * j + 2].rearrange("p h i j d -> p (h i j d)"), identh[:, :])
                last.then_inc(s_LT_ps, 1)
                if b >= 1:
                    pe.wait_ge(s_prob, H * b)
                for j in range(H // 2):
                    for t in range(TB):
                        last = tr(b16(sc_ps[0], F16)[:, j * N + t * P:j * N + (t + 1) * P],
                                  RS[:, b % 2, t, 2 * j:2 * j + 2].rearrange("p h i j d -> p (h i j d)"), identh[:, :])
                last.then_inc(s_RT_ps, 1)

            def attn_scores(b, h):
                pe.wait_ge(s_RT, 2 * b + 2)
                n = H * b + h
                if n >= 2:
                    pe.wait_ge(s_prob, n - 1)
                for t in range(TB):
                    last = mm(sc_ps[h % 2][:, t * N:(t + 1) * N], LT[:, h // 2, t * P:(t + 1) * P],
                              RT[:, h % 2, h // 2, :], start=True, stop=True)
                last.then_inc(s_score_ps, 1)

            def attn_context(b, g):
                pe.wait_ge(s_prob, H * b + 4 * g + 4)
                pe.wait_ge(s_LT, b + 1)
                for t in range(TB):
                    for j in range(4):
                        h = 4 * g + j
                        last = mm(attn_ps[32 * j:32 * j + 32, g * N:(g + 1) * N], PA[:, b % 2, t, h, :],
                                  EB_[:, h, t, :], start=(t == 0), stop=(t == TB - 1))
                last.then_inc(s_ctx_ps, 1)

            def attn_turn(b):
                pe.wait_ge(s_CT, b + 1)
                for t in range(TB):
                    for g in range(2):
                        last = tr(attn_ps[:, (2 * t + g) * P:(2 * t + g + 1) * P], CT[:, g * N + t * P:g * N + (t + 1) * P],
                                  ident[:, :])
                last.then_inc(s_CTT_ps, 1)
                if b == 0:
                    turn_w1()

            def attn_back(b):
                pe.wait_ge(s_ctx, b + 1)
                for t in range(TB):
                    last = tr(attn_ps[:, t * P:(t + 1) * P], CX[:, t, :], ident[:, :])
                last.then_inc(s_ctxT_ps, 1)

            def attn_combine(b):
                pe.wait_ge(s_ctxT, b + 1)
                for t in range(TB):
                    last = mm(attn_ps[:, t * C:(t + 1) * C], CXT[:, t * P:(t + 1) * P], wcT_sb[:, :], start=True, stop=True)
                last.then_inc(s_comb_ps, 1)

            def ffn_transpose(b):
                if b == 0:
                    pe.wait_ge(s_w2T, 1)
                if b:
                    pe.wait_ge(s_z2, b)
                pe.wait_ge(s_q_l, b + 1)
                for t in range(TB):
                    last = tr(b16(ffn_ps)[0:QK, t * P:(t + 1) * P], QS[:, b, t, :], identb[:, :])
                last.then_inc(s_qT_ps, 1)

            def ffn_hidden(b, half):
                pe.wait_ge(s_qT, b + 1)
                if b == 0:
                    pe.wait_ge(s_w1T, 1)
                if half:
                    pe.wait_ge(s_hid, 2 * b + 1)
                for i in range(2):
                    k = 2 * half + i
                    last = mm(ffn_ps[:, i * N:(i + 1) * N], w1T_sb[:, k * P:(k + 1) * P], QT[:, :], start=True, stop=True)
                last.then_inc(s_hid_ps, 1)

            def ffn_output(b):
                pe.wait_ge(s_hid, 2 * b + 2)
                for t in range(TB):
                    for k in range(FB):
                        last = mm(ffn_ps[:, t * C:(t + 1) * C], HID[:, k, t * P:(t + 1) * P], w2T_sb[:, k, :],
                                  start=(k == 0), stop=(k == FB - 1))
                last.then_inc(s_ffn_ps, 1)

            def moe_transpose(b):
                if b == 0:
                    pe.wait_ge(s_selT, 1)
                if b:
                    pe.wait_ge(s_out_sb, b)
                pe.wait_ge(s_xt, b + 1)
                for t in range(TB):
                    last = tr(moe_ps[:, t * P:(t + 1) * P], XTK[:, b % 2, t, :], ident[:, :])
                last.then_inc(s_xtT_ps, 1)

            def moe_select(b):
                pe.wait_ge(s_xtT, b + 1)
                for t in range(TB):
                    last = mm(moe_ps[:, t * E:(t + 1) * E], XTT[:, b % 2, t * P:(t + 1) * P], selT_sb[:, :],
                              start=True, stop=True)
                last.then_inc(s_sel_ps, 1)

            def moe_spread(b):
                pe.wait_ge(s_w_l, b + 1)
                if b == 0:
                    pe.wait_ge(s_zeroed, 2)
                pe.wait_ge(s_sel_e, b + 1)
                for t in range(TB):
                    last = tr(b16(moe_ps, F16)[0:3 * E, t * P:(t + 1) * P], WP[:, b, t].rearrange("p i e -> p (i e)"), identh[:, :])
                last.then_inc(s_wT_ps, 1)

            def moe_out(b, q):
                for i in range(2):
                    k = 2 * q + i
                    pe.wait_ge(s_hw, EB * b + k + 1)
                    for t in range(TB):
                        last = mm(moe_ps[:, t * C:(t + 1) * C], HWT[:, k % 4, t * P:(t + 1) * P], val_sb[:, k, :],
                                  start=(k == 0 and t == 0), stop=(k == EB - 1), skip_group_check=True)
                    last.then_inc(s_out_ps, 1)

            def moe_pair(b, q):
                if b == 0 and q == 0:
                    pe.wait_ge(w3_in, W3_LOADED)
                    pe.wait_ge(s_spread_set, 3)
                    pe.wait_ge(s_w1T, 1)
                    pe.wait_ge(s_b1, 1)
                for i in range(2):
                    k = 2 * q + i
                    n = EB * b + k
                    if n >= 2:
                        pe.wait_ge(s_hw, n - 1)
                    mm(hidden_ps[i][:, 0:N], keys_sb[:, k * EPB:(k + 1) * EPB, :].rearrange("p e h -> p (e h)"),
                       XTT[:, b % 2, :], start=True, stop=True)
                    if k == 0:
                        pe.wait_ge(s_wT, b + 1)
                    mm(hidden_ps[i][:, N:2 * N], spread[:, k, :], WT[:, b % 2, :], start=True, stop=True).then_inc(s_moe_ps, 1)
                if q:
                    moe_out(b, q - 1)

            def moe_output(b):
                moe_out(b, 3)

            run_steps({
                "conv_transpose": conv_transpose, "conv_project": conv_project, "conv_stack": conv_stack,
                "conv_scores": conv_scores, "conv_turn": conv_turn, "conv_output": conv_output,
                "attn_transpose": attn_transpose, "attn_scores": attn_scores, "attn_context": attn_context,
                "attn_turn": attn_turn, "attn_back": attn_back, "attn_combine": attn_combine,
                "ffn_transpose": ffn_transpose, "ffn_hidden": ffn_hidden, "ffn_output": ffn_output,
                "moe_transpose": moe_transpose, "moe_select": moe_select, "moe_spread": moe_spread,
                "moe_pair": moe_pair, "moe_output": moe_output,
            })

        @block.scalar
        def _(act):
            copy, fn = nc.scalar.copy, nc.scalar.activation
            act.dma_start(wv_sb[:, :], Wv).then_inc(w0_in, 16)
            act.dma_start(bh_sb[:, :], bh.rearrange("(d o) -> d o", o=1)).then_inc(w0_in, 16)
            act.dma_start(wproj[:, D:2 * D], Wg).then_inc(w_in, 16)
            act.dma_start(bfg[:, D:2 * D], bg.partition_broadcast(P)).then_inc(w_in, 16)
            act.dma_start(bv_b[:, :], bv.partition_broadcast(P)).then_inc(w_in, 16)

            def turn_weights():
                act.wait_ge(s_wcT_ps, 1)
                copy(wcT_sb[:, :], attn_ps[:, 0:P]).then_inc(s_wcT, 1)
                act.wait_ge(s_w2T_ps, 1)
                copy(w2T_sb[:, :, :].rearrange("p k c -> p (k c)"), ffn_ps[:, :]).then_inc(s_w2T, 1)
                act.wait_ge(s_selT_ps, 1)
                copy(selT_sb[:, :], moe_ps[:, 0:E]).then_inc(s_selT, 1)

            def conv_output(b):
                if b == 0:
                    turn_weights()

            def conv_transpose(b):
                act.wait_ge(s_xT_ps, b + 1)
                copy(XT[:, b % 2, :], conv_ps[:, 0:N]).then_inc(s_xT, 1)

            def conv_project(b):
                act.wait_ge(s_fg, b + 1)
                if b >= 2:
                    act.wait_ge(s_O_ps, b - 1)
                v = conv_ps[:, 0:TB * (2 * D + C)].rearrange("p (t k) -> p t k", t=TB)
                copy(HW[:, b % 2], v[:, :, 2 * D:2 * D + C]).then_inc(s_hW, 1)
                if b == 0:
                    act.wait_ge(s_phi_clamp, 1)
                    fn(phi_t[:, 5, :], phi_t[:, 4, :], ACT.Sin).then_inc(s_phi_cos, 1)

            def conv_scores(b):
                act.wait_ge(s_cmax, b + 1)
                if b >= 2:
                    act.wait_ge(s_ET_ps, b - 1)
                for t in range(TB):
                    last = fn(EA[:, b % 2, t, :], conv_ps[:, t * N:(t + 1) * N], ACT.Exp, bias=nmx[:, b, t:t + 1],
                              accum_out=den[:, b, t:t + 1])
                last.then_inc(s_cexp, 1)

            def proj_cos(b):
                act.wait_ge(s_y_clamp, b + 1)
                if b >= 2:
                    act.wait_ge(s_p_aug, 2 * (b - 1))
                fn(CS[:, b % 2], ARG[:, b % 2, 5], ACT.Sin).then_inc(s_y_cos, 1)

            def proj_split(b):
                act.wait_ge(s_p_aug, 2 * b + 2)
                if b >= 2:
                    act.wait_ge(s_LT_ps, b - 1)
                a = PA[:, b % 2].rearrange("p t h d -> p (t h) d")
                l = LS[:, b % 2].rearrange("p t h i j d -> p (t h) i j d")
                copy(l[:, :, 0], a[:, :, None, 0:DK].to_broadcast([P, TB * H, 2, DK])).then_inc(s_left_h, 1)

            def attn_scores(b, h):
                n = H * b + h
                act.wait_ge(s_score_ps, n + 1)
                if b >= 1:
                    act.wait_ge(s_ctx_ps, 2 * (b - 1) + h // 4 + 1)
                fn(EB_[:, h, :, :].rearrange("p t n -> p (t n)"), sc_ps[h % 2][:, :], ACT.Exp,
                   scale=1.0 / math.sqrt(DK)).then_inc(s_prob, 1)

            def attn_context(b, g):
                if g == 1:
                    act.wait_ge(s_ctx_ps, 2 * b + 2)
                    copy(CT[:, :], attn_ps[:, :]).then_inc(s_CT, 1)

            def attn_back(b):
                act.wait_ge(s_ctxT_ps, b + 1)
                copy(CXT[:, :], attn_ps[:, 0:N]).then_inc(s_ctxT, 1)
                if b == 0:
                    act.wait_ge(s_w1T_ps, 1)
                    copy(w1T_sb[:, :], b16(hidden_ps[0])[0:QK, 0:FF]).then_inc(s_w1T, 1)

            def ffn_cos(b):
                act.wait_ge(s_q_clamp, b + 1)
                fn(QC[:, b], QA[:, b % 2, 5], ACT.Sin).then_inc(s_q_cos, 1)

            def ffn_hidden(b, half):
                act.wait_ge(s_hid_ps, 2 * b + half + 1)
                if b >= 1:
                    act.wait_ge(s_ffn_ps, b)
                fn(HID[:, 2 * half:2 * half + 2, :].rearrange("p k n -> p (k n)"), ffn_ps[:, :], ACT.Relu).then_inc(s_hid, 1)

            def moe_transpose(b):
                act.wait_ge(s_xtT_ps, b + 1)
                copy(XTT[:, b % 2, :], moe_ps[:, 0:N]).then_inc(s_xtT, 1)

            def moe_select(b):
                act.wait_ge(s_sel_ps, b + 1)
                fn(SE[:, b].rearrange("p t e -> p (t e)"), moe_ps[:, 0:TB * E], ACT.Exp, scale=-1.0).then_inc(s_sel_e, 1)

            def moe_pair(b, q):
                for i in range(2):
                    k = 2 * q + i
                    n = EB * b + k
                    act.wait_ge(s_moe_ps, n + 1)
                    if n >= 4:
                        act.wait_ge(s_hw, n - 3)
                    fn(HR[:, k % 4, :], hidden_ps[i][:, 0:N], ACT.Relu).then_inc(s_relu, 1)

            run_steps({
                "conv_transpose": conv_transpose, "conv_project": conv_project, "conv_scores": conv_scores,
                "conv_output": conv_output, "proj_split": proj_split,
                "proj_cos": proj_cos, "attn_scores": attn_scores, "attn_context": attn_context, "attn_back": attn_back,
                "ffn_cos": ffn_cos, "ffn_hidden": ffn_hidden, "moe_transpose": moe_transpose,
                "moe_select": moe_select, "moe_pair": moe_pair,
            })

        @block.vector
        def _(dve):
            V = nc.vector

            def norm_stats(b, src, which, stats, mvs):
                for t in range(TB):
                    last = V.bn_stats(st[:, which, b, t, :], src[:, t, :])
                last.then_inc(stats, 1)
                dve.wait_ge(stats, b + 1)
                for t in range(TB):
                    last = V.bn_aggr(mv[:, which, b, t, :], st[:, which, b, t, :])
                last.then_inc(mvs, 1)

            def norm_apply(b, dst, src, which, rs, done):
                dve.wait_ge(rs, b + 1)
                for t in range(TB):
                    last = V.tensor_scalar(dst[:, t, :], src[:, t, :], mv[:, which, b, t, 0:1], rstd[:, which, b, t:t + 1],
                                           ALU.subtract, ALU.mult)
                last.then_inc(done, 1)

            def norm_affine(b, dst, tmp, src, which, mvs, rs, gain, plus, half, done):
                dve.wait_ge(mvs, b + 1)
                for t in range(TB):
                    V.scalar_tensor_tensor(out=tmp[:, t, :], in0=src[:, t, :], scalar=mv[:, which, b, t, 0:1],
                                           in1=gain, op0=ALU.subtract, op1=ALU.mult).then_inc(half, 1)
                dve.wait_ge(rs, b + 1)
                for t in range(TB):
                    dve.wait_ge(half, 2 * b + t + 1)
                    last = V.scalar_tensor_tensor(out=dst[:, t, :], in0=tmp[:, t, :], scalar=rstd[:, which, b, t:t + 1],
                                                  in1=plus[t], op0=ALU.mult, op1=ALU.add)
                last.then_inc(done, 1)

            dve.wait_ge(w0_in, W0_LOADED)
            V.tensor_copy(bh_row[:, :], bh_sb[:, 0:1].to_broadcast([D, P])).then_inc(s_bh_row, 1)
            dve.wait_ge(s_whT_ps, 1)
            V.tensor_copy(whT_sb[:, :], hidden_ps[0][0:D, 0:P]).then_inc(s_whT, 1)
            dve.wait_ge(s_wv_ps, 1)
            V.tensor_copy(wproj[:, 2 * D:2 * D + C], hidden_ps[1][:, 0:C]).then_inc(s_wproj_sb, 1)
            dve.wait_ge(w_in, W_LOADED)
            dve.wait_ge(s_rc_ps, 1)
            V.scalar_tensor_tensor(out=rc[:, :], in0=sc_ps[0][:, 0:C], scalar=gam[:, 0:1], in1=bv_b[:, :],
                                   op0=ALU.mult, op1=ALU.add).then_inc(s_rc, 1)

            def reduce_phi():
                dve.wait_ge(w1_in, W1_LOADED)
                V.tensor_scalar(phi_t[:, 0, :], phi_b[:, :], math.pi / 2, None, ALU.add).then_inc(s_phi_step, 1)
                dve.wait_ge(s_phi_step, 1)
                V.tensor_scalar(phi_t[:, 1, :], phi_t[:, 0, :], 0.5 / math.pi, ROUND, ALU.mult, ALU.add).then_inc(s_phi_step, 1)
                dve.wait_ge(s_phi_step, 2)
                V.tensor_scalar(phi_t[:, 2, :], phi_t[:, 1, :], ROUND, None, ALU.subtract).then_inc(s_phi_step, 1)
                dve.wait_ge(s_phi_step, 3)
                V.scalar_tensor_tensor(out=phi_t[:, 3, :], in0=phi_t[:, 2, :], scalar=-TWO_PI_HI, in1=phi_t[:, 0, :],
                                       op0=ALU.mult, op1=ALU.add).then_inc(s_phi_step, 1)
                dve.wait_ge(s_phi_step, 4)
                V.scalar_tensor_tensor(out=phi_t[:, 1, :], in0=phi_t[:, 2, :], scalar=-TWO_PI_LO, in1=phi_t[:, 3, :],
                                       op0=ALU.mult, op1=ALU.add).then_inc(s_phi_step, 1)
                dve.wait_ge(s_phi_step, 5)
                V.tensor_scalar(phi_t[:, 4, :], phi_t[:, 1, :], PI_F32, -PI_F32, ALU.min, ALU.max).then_inc(s_phi_clamp, 1)

            def conv_project(b):
                dve.wait_ge(s_proj_ps, b + 1)
                v = conv_ps[:, 0:TB * (2 * D + C)].rearrange("p (t k) -> p t k", t=TB)
                V.tensor_tensor(FGs[:, b], v[:, :, 0:2 * D], bfg[:, None, :].to_broadcast([P, TB, 2 * D]), ALU.add).then_inc(s_fg, 1)
                if b == 0:
                    reduce_phi()

            def conv_stack(b):
                dve.wait_ge(s_stack_ps, b + 1)
                if b >= 2:
                    dve.wait_ge(s_cscore_ps, b - 1)
                V.tensor_copy(FGT[:, b % 2, :], b16(conv_ps)[:, 0:2 * N]).then_inc(s_stack, 1)

            def conv_scores(b):
                dve.wait_ge(s_cscore_ps, b + 1)
                V.tensor_reduce(nmx[:, b, :], conv_ps[:, :].rearrange("p (t n) -> p t n", t=TB), AX.X, ALU.max,
                                negate=True).then_inc(s_cmax, 1)

            def conv_turn(b):
                dve.wait_ge(s_ET_ps, b + 1)
                if b >= 2:
                    dve.wait_ge(s_O_ps, b - 1)
                V.tensor_copy(ETs[:, b % 2].rearrange("p t n -> p (t n)"), conv_ps[:, :]).then_inc(s_ET, 1)
                dve.wait_ge(s_cexp, b + 1)
                V.reciprocal(rden[:, b, :], den[:, b, :]).then_inc(s_crden, 1)
                dve.wait_ge(s_crden, b + 1)
                V.tensor_scalar(gden[:, b, :], rden[:, b, :], gam[:, 0:1], None, ALU.mult).then_inc(s_cgain, 1)

            def conv_output(b):
                dve.wait_ge(s_O_ps, b + 1)
                dve.wait_ge(s_xr, b + 1)
                dve.wait_ge(s_cgain, b + 1)
                for t in range(TB):
                    last = V.scalar_tensor_tensor(out=T0[:, b, t, :], in0=conv_ps[:, t * C:(t + 1) * C],
                                                  scalar=gden[:, b, t:t + 1], in1=XR[:, b, t, :], op0=ALU.mult, op1=ALU.add)
                last.then_inc(s_t0, 1)

            def proj_norm(b):
                dve.wait_ge(s_t0, b + 1)
                norm_stats(b, T0[:, b], 0, s_y_stats, s_y_mv)
                if b == 0:
                    dve.wait_ge(s_b1T_ps, 1)
                    V.tensor_copy(w1_c[:, :, NQ], hidden_ps[1][:, 0:FB]).then_inc(s_b1, 1)
                    dve.wait_ge(w2_in, W2_LOADED)
                    V.tensor_scalar(theta2[:, :], theta_b[:, :], math.pi / 2, None, ALU.add).then_inc(s_theta2, 1)

            def proj_angle(b):
                if b >= 2:
                    dve.wait_ge(s_y_bias, b - 1)
                norm_apply(b, Y[:, b % 2], T0[:, b], 0, s_y_rstd, s_y)

            def proj_reduce(b):
                dve.wait_ge(s_y_k, b + 1)
                if b >= 2:
                    dve.wait_ge(s_y_clamp, b - 1)
                A = ARG[:, b % 2]
                V.scalar_tensor_tensor(out=A[:, 3], in0=A[:, 2], scalar=-TWO_PI_HI, in1=A[:, 0],
                                       op0=ALU.mult, op1=ALU.add).then_inc(s_y_r1, 1)
                dve.wait_ge(s_y_r1, b + 1)
                V.scalar_tensor_tensor(out=A[:, 4], in0=A[:, 2], scalar=-TWO_PI_LO, in1=A[:, 3],
                                       op0=ALU.mult, op1=ALU.add).then_inc(s_y_r2, 1)
                dve.wait_ge(s_y_r2, b + 1)
                if b >= 2:
                    dve.wait_ge(s_y_cos, b - 1)
                V.tensor_scalar(A[:, 5], A[:, 4], PI_F32, -PI_F32, ALU.min, ALU.max).then_inc(s_y_clamp, 1)

            def proj_cos(b):
                dve.wait_ge(s_y_cos, b + 1)
                if b >= 2:
                    dve.wait_ge(s_p_aug, 2 * (b - 1))
                dve.wait_ge(s_const_set, 2)
                V.tensor_tensor_scan(SC[:, b % 2].rearrange("p t c -> p (t c)"), scanmask[:, :],
                                     CS[:, b % 2].rearrange("p t c -> p (t c)"), 1.0, ALU.max, ALU.mult).then_inc(s_scan, 1)

            def proj_split(b):
                dve.wait_ge(s_left_h, b + 1)
                V.tensor_tensor(LS[:, b % 2, :, :, 1].rearrange("p t h j d -> p (t h) j d"),
                                PA[:, b % 2, :, :, None, 0:DK].rearrange("p t h j d -> p (t h) j d").to_broadcast([P, TB * H, 2, DK]),
                                LS[:, b % 2, :, :, 0].rearrange("p t h j d -> p (t h) j d"), ALU.subtract).then_inc(s_left_l, 1)

            def attn_transpose(b):
                dve.wait_ge(s_LT_ps, b + 1)
                if b >= 1:
                    dve.wait_ge(s_score_ps, H * b)
                V.tensor_copy(LT[:, :, :].rearrange("p j n -> p (j n)"), b16(attn_ps, F16)).then_inc(s_LT, 1)
                dve.wait_ge(s_RT_ps, b + 1)
                dve.wait_ge(s_zeroed, 1)
                for i in range(2):
                    q = slice(64 * i, 64 * i + 64)
                    V.tensor_copy(RT[q, i, :, :].rearrange("p j n -> p (j n)"), b16(sc_ps[0], F16)[q, :]).then_inc(s_RT, 1)

            def attn_turn(b):
                dve.wait_ge(s_CTT_ps, b + 1)
                v = attn_ps[:, :].rearrange("p (k d) -> p k d", d=32)
                V.reciprocal(ard[:, :], v[:, :, DK]).then_inc(s_arden, 1)
                dve.wait_ge(s_arden, b + 1)
                V.tensor_tensor(CX[:, :, :].rearrange("p t (h d) -> p (t h) d", d=DK), v[:, :, 0:DK],
                                ard[:, :, None].to_broadcast([P, 2 * H, DK]), ALU.mult).then_inc(s_ctx, 1)

            def attn_combine(b):
                dve.wait_ge(s_comb_ps, b + 1)
                dve.wait_ge(s_y_bias, b + 1)
                V.tensor_tensor(Z[:, b % 2], tb_of(attn_ps[:, 0:TB * C]), YB[:, b % 4], ALU.add).then_inc(s_z, 1)

            def ffn_norm(b):
                dve.wait_ge(s_z, b + 1)
                norm_stats(b, Z[:, b % 2], 1, s_z_stats, s_z_mv)
                if b >= 2:
                    dve.wait_ge(s_x1_bias, b - 1)
                    dve.wait_ge(s_q_arg, b - 1)
                norm_affine(b, X1[:, b % 2], ZN[:, b % 2], Z[:, b % 2], 1, s_z_mv, s_z_rstd, g1_b[:, :],
                            [be1_b[:, :]] * TB, s_z_n, s_x1)

            def ffn_angle(b):
                dve.wait_ge(s_q_k, b + 1)
                A = QA[:, b % 2]
                V.scalar_tensor_tensor(out=A[:, 3], in0=A[:, 2], scalar=-TWO_PI_HI, in1=A[:, 0],
                                       op0=ALU.mult, op1=ALU.add).then_inc(s_q_r1, 1)
                dve.wait_ge(s_q_r1, b + 1)
                V.scalar_tensor_tensor(out=A[:, 4], in0=A[:, 2], scalar=-TWO_PI_LO, in1=A[:, 3],
                                       op0=ALU.mult, op1=ALU.add).then_inc(s_q_r2, 1)
                dve.wait_ge(s_q_r2, b + 1)
                if b >= 2:
                    dve.wait_ge(s_q_cos, b - 1)
                V.tensor_scalar(A[:, 5], A[:, 4], PI_F32, -PI_F32, ALU.min, ALU.max).then_inc(s_q_clamp, 1)

            def ffn_transpose(b):
                dve.wait_ge(s_qT_ps, b + 1)
                if b >= 1:
                    dve.wait_ge(s_hid_ps, 2 * b)
                V.tensor_copy(QT[:, :], b16(ffn_ps)[0:QK, 0:N]).then_inc(s_qT, 1)

            def ffn_output(b):
                dve.wait_ge(s_ffn_ps, b + 1)
                dve.wait_ge(s_x1_bias, b + 1)
                V.tensor_tensor(Z2[:, b % 2], tb_of(ffn_ps[:, 0:TB * C]), X1B[:, b % 2], ALU.add).then_inc(s_z2, 1)

            def norm_second(b):
                dve.wait_ge(s_z2, b + 1)
                norm_stats(b, Z2[:, b % 2], 2, s_n_stats, s_n_mv)
                dve.wait_ge(s_t0_bias, b + 1)
                norm_affine(b, T1[:, b], NN[:, b % 2], Z2[:, b % 2], 2, s_n_mv, s_n_rstd, g2_b[:, :],
                            [T0B[:, b % 2, t, :] for t in range(TB)], s_n_n, s_t1)

            def norm_third(b):
                dve.wait_ge(s_t1, b + 1)
                norm_stats(b, T1[:, b], 3, s_u_stats, s_u_mv)
                if b >= 2:
                    dve.wait_ge(s_xtT_ps, b - 1)
                norm_apply(b, XTK[:, b % 2], T1[:, b], 3, s_u_rstd, s_xt)

            def moe_select(b):
                dve.wait_ge(s_sel_e, b + 1)
                V.tensor_scalar(SE[:, b], SE[:, b], 1.0, 1.0 / W_SCALE, ALU.add, ALU.mult).then_inc(s_sel_1, 1)
                dve.wait_ge(s_sel_1, b + 1)
                V.reciprocal(SG[:, b, :, 0:E], SE[:, b]).then_inc(s_sel_s, 1)
                dve.wait_ge(s_sel_s, b + 1)
                for t in range(TB):
                    last = V.max(V8[:, b, t, :], SG[:, b, t, 0:E])
                last.then_inc(s_top8, 1)

            def moe_topk(b):
                dve.wait_ge(s_top8, b + 1)
                dve.wait_ge(s_const_set, 5)
                V.tensor_copy(R8[:, b, :, 0:2], V8[:, b, :, 0:2]).then_inc(s_top2, 1)
                dve.wait_ge(s_top2, b + 1)
                for t in range(TB):
                    last = V.match_replace(SR[:, b, t, :], R8[:, b, t, :], SG[:, b, t, :], 0.0)
                last.then_inc(s_rest, 1)

            def moe_spread(b):
                dve.wait_ge(s_wT_ps, b + 1)
                if b >= 2:
                    dve.wait_ge(s_moe_ps, EB * (b - 1))
                V.tensor_copy(WT[:, b % 2, :], b16(moe_ps, F16)[0:3 * E, 0:N]).then_inc(s_wT, 1)

            def moe_pair(b, q):
                for i in range(2):
                    k = 2 * q + i
                    n = EB * b + k
                    dve.wait_ge(s_relu, n + 1)
                    if n >= 4:
                        dve.wait_ge(s_out_ps, n - 3)
                    V.tensor_tensor(HWT[:, k % 4, :], hidden_ps[i][:, N:2 * N], HR[:, k % 4, :], ALU.mult).then_inc(s_hw, 1)

            def moe_output(b):
                dve.wait_ge(s_out_ps, EB * (b + 1))
                if b >= 2:
                    dve.wait_ge(stored[b % 2], 16 * (b // 2))
                V.tensor_tensor(OB[:, b % 2], tb_of(moe_ps[:, 0:TB * C]), T1[:, b], ALU.add).then_inc(s_out_sb, 1)

            run_steps({
                "conv_project": conv_project, "conv_stack": conv_stack, "conv_scores": conv_scores,
                "conv_turn": conv_turn, "conv_output": conv_output, "proj_norm": proj_norm, "proj_angle": proj_angle,
                "proj_reduce": proj_reduce, "proj_cos": proj_cos, "proj_split": proj_split,
                "attn_transpose": attn_transpose, "attn_turn": attn_turn, "attn_combine": attn_combine,
                "ffn_norm": ffn_norm, "ffn_angle": ffn_angle, "ffn_transpose": ffn_transpose, "ffn_output": ffn_output,
                "norm_second": norm_second, "norm_third": norm_third, "moe_select": moe_select, "moe_topk": moe_topk,
                "moe_spread": moe_spread, "moe_pair": moe_pair, "moe_output": moe_output,
            })

        @block.gpsimd
        def _(pool):
            G = nc.gpsimd
            for m in (ident, identb, identh):
                G.memset(m[:, :], 0.0).then_inc(s_ident, 1)
            pool.wait_ge(s_ident, 3)
            for m in (ident, identb, identh):
                G.affine_select(out=m[:, :], in_=m[:, :], compare_op=ALU.not_equal, fill=1.0, base=0,
                                pattern=[[-1, P]], channel_multiplier=1).then_inc(s_ident, 1)
            G.memset(minushalf[:, :], -0.5).then_inc(s_ones_set, 1)
            G.memset(PA[:, :, :, :, DK:32], 1.0).then_inc(s_ones_set, 1)
            G.memset(QS[:, :, :, 9 * NQ:QK], 1.0).then_inc(s_ones_set, 1)
            pool.wait_ge(s_ones_set, 3)

            def set_attention_constants():
                G.memset(scanmask[:, :], -2.0).then_inc(s_const_set, 1)
                pool.wait_ge(s_const_set, 1)
                G.memset(scanmask[:, :].rearrange("p (g d) -> p g d", d=DK)[:, :, 1:2], 1.0).then_inc(s_const_set, 1)
                G.memset(RT[:, :, :, :], 0.0).then_inc(s_zeroed, 1)

            def set_moe_constants():
                G.memset(spread[:, :, :], 0.0).then_inc(s_const_set, 1)
                G.memset(WP[:, :, :, 2, :], 0.0).then_inc(s_zeroed, 1)
                G.memset(SG[:, :, :, E:E + 6], -1.0).then_inc(s_const_set, 1)
                G.memset(R8[:, :, :, 2:8], -1.0).then_inc(s_const_set, 1)
                pool.wait_ge(s_const_set, 3)
                for i in range(3):
                    if i:
                        pool.wait_ge(s_spread_set, i)
                    v = spread[i * E:(i + 1) * E, :, :].rearrange("p k (e h) -> p k e h", e=EPB)
                    G.affine_select(out=v, in_=v, compare_op=ALU.not_equal, fill=1.0 / W_SCALE, base=0,
                                    pattern=[[-EPB, EB], [-1, EPB], [0, HE]], channel_multiplier=1).then_inc(s_spread_set, 1)
                pool.wait_ge(s_spread_set, 3)

            def rsqrt(b, which, mvs, vs, rs):
                pool.wait_ge(mvs, b + 1)
                G.tensor_scalar(var[:, which, b, :], mv[:, which, b, :, 1], EPS, 1.0, ALU.add, ALU.mult).then_inc(vs, 1)
                pool.wait_ge(vs, b + 1)
                G.tensor_tensor(rstd[:, which, b, :], var[:, which, b, :], minushalf[:, :], ALU.pow).then_inc(rs, 1)

            def reduce_angle(b, A, a, k1, k):
                pool.wait_ge(a, b + 1)
                G.tensor_scalar(A[:, 1], A[:, 0], 0.5 / math.pi, ROUND, ALU.mult, ALU.add).then_inc(k1, 1)
                pool.wait_ge(k1, b + 1)
                G.tensor_scalar(A[:, 2], A[:, 1], -ROUND, 1.0, ALU.add, ALU.mult).then_inc(k, 1)

            def stack_w1():
                pool.wait_ge(w1_in, W1_LOADED)
                pool.wait_ge(s_phi_cos, 1)
                G.tensor_tensor(w1_c[:, :, 0:NQ], w1_sb[:, :, :], phi_t[:, 5:6, :].to_broadcast([P, FB, NQ]),
                                ALU.mult).then_inc(s_w1_step, 1)
                pool.wait_ge(s_b1, 1)
                pool.wait_ge(s_w1_step, 1)
                G.tensor_copy(w1_p[:, :, 0, :], w1_c[:, :, :]).then_inc(s_w1_step, 1)
                pool.wait_ge(s_w1_step, 2)
                G.tensor_tensor(w1_r[:, :, :], w1_c[:, :, :], w1_p[:, :, 0, :], ALU.subtract).then_inc(s_w1_step, 1)
                pool.wait_ge(s_w1_step, 3)
                G.tensor_copy(w1_p[:, :, 1, :], w1_r[:, :, :]).then_inc(s_w1_step, 1)
                pool.wait_ge(s_w1_step, 4)
                G.tensor_tensor(w1_p[:, :, 2, :], w1_r[:, :, :], w1_p[:, :, 1, :], ALU.subtract).then_inc(s_w1_step, 1)
                pool.wait_ge(s_w1_step, 5)
                for k in range(FB):
                    G.tensor_copy(w1_st[:, k, 0:9 * NQ].rearrange("p (i j q) -> p i j q", i=3, j=3),
                                  w1_p[:, k, None, :, 0:NQ].to_broadcast([P, 3, 3, NQ])).then_inc(s_w1_stack, 1)
                G.tensor_copy(w1_st[:, :, 9 * NQ:QK], w1_p[:, :, :, NQ]).then_inc(s_w1_stack, 1)

            def conv_scores(b):
                pool.wait_ge(x_in[b], 16)
                pool.wait_ge(s_rc, 1)
                G.tensor_tensor(XR[:, b], X[:, b], rc[:, None, :].to_broadcast([P, TB, C]), ALU.add).then_inc(s_xr, 1)
                if b == 0:
                    set_attention_constants()

            def conv_project(b):
                pool.wait_ge(s_fg, b + 1)
                if b >= 2:
                    pool.wait_ge(s_stack_ps, b - 1)
                st_f = FGp[:, b % 2, :, 0].rearrange("p t (i j) d -> p t i j d", i=3)
                st_g = FGp[:, b % 2, :, 1].rearrange("p t (i j) d -> p t i j d", i=3)

                def three(src, side):
                    return src[:, :, None, side * D:(side + 1) * D].to_broadcast([P, TB, 3, D])
                G.tensor_copy(st_f[:, :, 0], three(FGs[:, b], 0)).then_inc(s_fg_h, 1)
                G.tensor_copy(st_g[:, :, :, 0], three(FGs[:, b], 1)).then_inc(s_fg_h, 1)
                pool.wait_ge(s_fg_h, 2 * b + 2)
                G.tensor_tensor(FGr[:, b].rearrange("p t (s d) -> p t s d", s=2), FGs[:, b].rearrange("p t (s d) -> p t s d", s=2),
                                FGp[:, b % 2, :, :, 0], ALU.subtract).then_inc(s_fg_r, 1)
                pool.wait_ge(s_fg_r, b + 1)
                G.tensor_copy(st_f[:, :, 1], three(FGr[:, b], 0)).then_inc(s_fg_m, 1)
                G.tensor_copy(st_g[:, :, :, 1], three(FGr[:, b], 1)).then_inc(s_fg_m, 1)
                pool.wait_ge(s_fg_m, 2 * b + 2)
                G.tensor_tensor(st_f[:, :, 2], three(FGr[:, b], 0), st_f[:, :, 1], ALU.subtract).then_inc(s_fg_l, 1)
                G.tensor_tensor(st_g[:, :, :, 2], three(FGr[:, b], 1), st_g[:, :, :, 1], ALU.subtract).then_inc(s_fg_l, 1)

            def proj_norm(b):
                rsqrt(b, 0, s_y_mv, s_y_var, s_y_rstd)

            def proj_angle(b):
                pool.wait_ge(s_y, b + 1)
                if b == 0:
                    pool.wait_ge(s_theta2, 1)
                    pool.wait_ge(w2_in, W2_LOADED)
                if b >= 2:
                    pool.wait_ge(s_y_r2, b - 1)
                G.tensor_tensor(ARG[:, b % 2, 0].rearrange("p t (h d) -> p (t h) d", d=DK),
                                Y[:, b % 2].rearrange("p t (h d) -> p (t h) d", d=DK),
                                theta2[:, None, :].to_broadcast([P, TB * H, DK]), ALU.add).then_inc(s_y_arg, 1)
                reduce_angle(b, ARG[:, b % 2], s_y_arg, s_y_k1, s_y_k)
                if b >= 4:
                    pool.wait_ge(s_z, b - 3)
                G.tensor_tensor(YB[:, b % 4], Y[:, b % 2], bc_b[:, None, :].to_broadcast([P, TB, C]), ALU.add).then_inc(s_y_bias, 1)

            def proj_split(b):
                pool.wait_ge(s_scan, b + 1)
                if b >= 2:
                    pool.wait_ge(s_ctx_ps, 2 * (b - 1))
                    pool.wait_ge(s_RT_ps, b - 1)
                q = SC[:, b % 2].rearrange("p t (h d) -> p (t h) d", d=DK)
                c = CS[:, b % 2].rearrange("p t (h d) -> p (t h) d", d=DK)
                a = PA[:, b % 2].rearrange("p t h d -> p (t h) d")
                G.tensor_tensor(a[:, :, 1:DK], q[:, :, 1:DK], c[:, :, 0:1].to_broadcast([P, TB * H, DK - 1]), ALU.mult).then_inc(s_p_aug, 1)
                G.tensor_copy(a[:, :, 0:1], q[:, :, DK - 1:DK]).then_inc(s_p_aug, 1)
                l = LS[:, b % 2].rearrange("p t h i j d -> p (t h) (i j d)").bitcast(U32).rearrange("p k (i j d) -> p k i j d", i=2, j=2)
                r = RS[:, b % 2].rearrange("p t h i j d -> p (t h) (i j d)").bitcast(U32).rearrange("p k (i j d) -> p k i j d", i=2, j=2)
                pool.wait_ge(s_left_h, b + 1)
                G.tensor_copy(r[:, :, :, 0], l[:, :, 0]).then_inc(s_right, 1)
                pool.wait_ge(s_left_l, b + 1)
                G.tensor_copy(r[:, :, :, 1], l[:, :, 1]).then_inc(s_right, 1)
                if b == 0:
                    stack_w1()

            def attn_scores(b, h):
                if b == 0 and h == 0:
                    set_moe_constants()

            def ffn_norm(b):
                rsqrt(b, 1, s_z_mv, s_z_var, s_z_rstd)
                pool.wait_ge(s_x1, b + 1)
                if b >= 2:
                    pool.wait_ge(s_q_r2, b - 1)
                G.tensor_scalar(QA[:, b % 2, 0], X1[:, b % 2, :, 0:NQ], math.pi / 2, 1.0, ALU.add, ALU.mult).then_inc(s_q_arg, 1)
                reduce_angle(b, QA[:, b % 2], s_q_arg, s_q_k1, s_q_k)
                if b >= 2:
                    pool.wait_ge(s_z2, b - 1)
                G.tensor_tensor(X1B[:, b % 2], X1[:, b % 2], b2_b[:, None, :].to_broadcast([P, TB, C]), ALU.add).then_inc(s_x1_bias, 1)

            def ffn_cos(b):
                v = QS[:, b, :, 0:9 * NQ].rearrange("p t (i j q) -> p t i j q", i=3, j=3)

                def three(src):
                    return src[:, :, None, :].to_broadcast([P, TB, 3, NQ])
                pool.wait_ge(s_q_cos, b + 1)
                G.tensor_copy(v[:, :, 0], three(QC[:, b])).then_inc(s_q_h, 1)
                pool.wait_ge(s_q_h, b + 1)
                G.tensor_tensor(QR[:, b], QC[:, b], v[:, :, 0, 0], ALU.subtract).then_inc(s_q_r, 1)
                pool.wait_ge(s_q_r, b + 1)
                G.tensor_copy(v[:, :, 1], three(QR[:, b])).then_inc(s_q_m, 1)
                pool.wait_ge(s_q_m, b + 1)
                G.tensor_tensor(v[:, :, 2], three(QR[:, b]), v[:, :, 1], ALU.subtract).then_inc(s_q_l, 1)

            def norm_second(b):
                if b >= 2:
                    pool.wait_ge(s_t1, b - 1)
                G.tensor_tensor(T0B[:, b % 2], T0[:, b], be2_b[:, None, :].to_broadcast([P, TB, C]), ALU.add).then_inc(s_t0_bias, 1)
                rsqrt(b, 2, s_n_mv, s_n_var, s_n_rstd)

            def norm_third(b):
                rsqrt(b, 3, s_u_mv, s_u_var, s_u_rstd)

            def moe_topk(b):
                pool.wait_ge(s_rest, b + 1)
                G.tensor_tensor(W[:, b], SG[:, b, :, 0:E], SR[:, b, :, 0:E], ALU.subtract).then_inc(s_w, 1)
                pool.wait_ge(s_w, b + 1)
                G.tensor_copy(WP[:, b, :, 0, :], W[:, b]).then_inc(s_w_h, 1)
                pool.wait_ge(s_w_h, b + 1)
                G.tensor_tensor(WP[:, b, :, 1, :], W[:, b], WP[:, b, :, 0, :], ALU.subtract).then_inc(s_w_l, 1)

            run_steps({
                "conv_project": conv_project, "conv_scores": conv_scores,
                "proj_norm": proj_norm, "proj_angle": proj_angle, "proj_split": proj_split, "attn_scores": attn_scores,
                "ffn_norm": ffn_norm, "ffn_cos": ffn_cos,
                "norm_second": norm_second, "norm_third": norm_third, "moe_topk": moe_topk,
            })


_INS = ["x", "L0_conv_Wf", "L0_conv_bf", "L0_conv_Wg", "L0_conv_bg", "L0_conv_Wh", "L0_conv_bh", "L0_conv_Wv",
        "L0_conv_bv", "L0_conv_gamma", "L1_attn_theta_attn", "L1_attn_phi_ffn", "L1_attn_W_comb", "L1_attn_b_comb",
        "L1_attn_W1", "L1_attn_b1", "L1_attn_W2", "L1_attn_b2", "L1_attn_ln1_g", "L1_attn_ln1_b", "L1_attn_ln2_g",
        "L1_attn_ln2_b", "L1_ffn_expert_sel", "L1_ffn_keys", "L1_ffn_values"]


def kernel(**inputs):
    import numpy as _np
    import concourse.bacc as _bacc
    from concourse import mybir as _mybir
    from concourse.bass_utils import run_bass_kernel_spmd as _run

    nc = _bacc.Bacc("TRN2", target_bir_lowering=False, num_devices=1)
    arrays, args = {}, []
    for name in _INS:
        a = _np.ascontiguousarray(inputs[name])
        arrays[f"in_{name}"] = a
        args.append(nc.dram_tensor(f"in_{name}", a.shape, _mybir.dt.from_np(a.dtype), kind="ExternalInput").ap())
    x = inputs["x"]
    args.append(nc.dram_tensor("out_0", x.shape, _mybir.dt.from_np(_np.dtype("float32")), kind="ExternalOutput").ap())
    build(nc, *args)
    r = _run(nc, [arrays], core_ids=[0])
    return r.results[0]["out_0"]
```
